# Optimizing a Trainium2 kernel written in Bass

```python
import numpy as np
import jax
import jax.numpy as jnp

def _softmax(x, axis=-1):
    return jax.nn.softmax(x, axis=axis)

def _gelu(x):
    return jax.nn.gelu(x, approximate=True)

def _silu(x):
    return jax.nn.silu(x)

def _sigmoid(x):
    return jax.nn.sigmoid(x)

def _layernorm(x, axis=-1, eps=1e-05):
    m = jnp.mean(x, axis=axis, keepdims=True)
    v = jnp.var(x, axis=axis, keepdims=True)
    return (x - m) / jnp.sqrt(v + eps)

def _scatter_add(tgt, idx, src, axis=0):
    return tgt.at[idx].add(src)

def _segment_sum(src, seg, n):
    return jax.ops.segment_sum(src, seg, n)
kernel_name = 'mk_rec_standalone_d1_rec_r8_b27c3e'

def setup_inputs(seed: int=0):
    np.random.seed(seed)
    _w = jnp.asarray

    def _rec_inputs():
        import jax
        import jax.numpy as jnp
        _rk = jax.random.key(seed)
        r_x = -0.000392918 + 0.999932 * jax.random.normal(jax.random.fold_in(_rk, 1), (2048, 256, 32), jnp.float32)
        r_y = jax.random.uniform(jax.random.fold_in(_rk, 2), (2048, 256), jnp.float32, 0.0, 0.999998)
        r_error0 = jax.random.uniform(jax.random.fold_in(_rk, 3), (2048,), jnp.float32, 0.0, 0.999706)
        r_gate0 = jax.random.uniform(jax.random.fold_in(_rk, 4), (2048, 8), jnp.float32, 0.0, 0.241025)
        return (r_x, r_y, r_error0, r_gate0)
    r_x, r_y, r_error0, r_gate0 = _rec_inputs()

    def _L0_rec_setup():
        import jax, jax.numpy as jnp
        import numpy as np
        MEM, C, S, T_TRAJ, D_IN, H, ENC = (20, 8, 32, 24, 32, 16, 64)
        B, T = (256, 256)

        def _lstm_cell(xt, h, c, wih, whh, b):
            g = xt @ wih + h @ whh + b
            i, f, gg, o = jnp.split(g, 4, axis=1)
            c = jax.nn.sigmoid(f) * c + jax.nn.sigmoid(i) * jnp.tanh(gg)
            h = jax.nn.sigmoid(o) * jnp.tanh(c)
            return (h, c)

        def _clamp01(t):
            return jax.nn.relu(t) - jax.nn.relu(t - 1.0)

        def _forward(x, y, error0, gate0, We, Ue, be, Wx, Ws, bk, enc_w1, enc_b1, enc_w2, enc_b2, gate_w, gate_b, lstm_wih1, lstm_whh1, lstm_b1, lstm_wih2, lstm_whh2, lstm_b2):
            b = x.shape[0]
            mem0 = jnp.zeros((b, MEM, T_TRAJ + 1), x.dtype).at[:, :, -1].set(0.5)
            zS = jnp.zeros((b, S), x.dtype)
            zH = jnp.zeros((b, H), x.dtype)
            carry0 = (zS, error0, gate0, mem0, zH, zH, zH, zH)

            def step(carry, xy):
                xt, yt = xy
                st, err, gs, mem, h1, c1, h2, c2 = carry
                encoded = jnp.tanh(xt @ We + st @ Ue + be)
                new_state = jnp.tanh(jnp.einsum('bd,cds->bcs', xt, Wx) + jnp.einsum('bs,cst->bct', st, Ws) + bk)
                inp = jnp.concatenate([encoded, err[:, None]], axis=1)
                mem = jnp.concatenate([inp[:, None, :], mem[:, :-1, :]], axis=1)
                a = jax.nn.relu(mem.reshape(b, -1) @ enc_w1 + enc_b1)
                agent_in = jax.nn.relu(a @ enc_w2 + enc_b2)
                h1, c1 = _lstm_cell(agent_in, h1, c1, lstm_wih1, lstm_whh1, lstm_b1)
                h2, c2 = _lstm_cell(h1, h2, c2, lstm_wih2, lstm_whh2, lstm_b2)
                gate = jax.nn.softmax(h2 @ gate_w + gate_b, axis=1)
                theta = _clamp01(jnp.mean(jnp.abs(mem[:, :10, -1]), axis=1) * 2.5)[:, None]
                gate = gate * theta + gs * (1.0 - theta)
                st = jnp.einsum('bc,bcs->bs', gate, new_state)
                pred = _clamp01(st[:, -1])
                err = pred - yt
                return ((st, err, gate, mem, h1, c1, h2, c2), pred)
            _, preds = jax.lax.scan(step, carry0, (jnp.swapaxes(x, 0, 1), jnp.swapaxes(y, 0, 1)))
            return jnp.swapaxes(preds, 0, 1)
        key = jax.random.key(seed)
        ks = jax.random.split(key, 16)
        rn = lambda k, shape, s: jax.random.normal(k, shape, jnp.float32) * s
        return {'x': jax.random.normal(ks[0], (B, T, D_IN), jnp.float32), 'y': jax.random.uniform(ks[1], (B, T), dtype=jnp.float32), 'error0': jax.random.uniform(ks[2], (B,), dtype=jnp.float32), 'gate0': jax.nn.softmax(jax.random.uniform(ks[3], (B, C), dtype=jnp.float32), axis=1), 'We': rn(ks[4], (D_IN, T_TRAJ), 0.15), 'Ue': rn(ks[5], (S, T_TRAJ), 0.15), 'be': jnp.zeros((T_TRAJ,), jnp.float32), 'Wx': rn(ks[6], (C, D_IN, S), 0.15), 'Ws': rn(ks[7], (C, S, S), 0.15), 'bk': jnp.zeros((C, S), jnp.float32), 'enc_w1': rn(ks[8], (MEM * (T_TRAJ + 1), ENC), 0.05), 'enc_b1': jnp.zeros((ENC,), jnp.float32), 'enc_w2': rn(ks[9], (ENC, H), 0.1), 'enc_b2': jnp.zeros((H,), jnp.float32), 'gate_w': rn(ks[10], (H, C), 0.2), 'gate_b': jnp.zeros((C,), jnp.float32), 'lstm_wih1': rn(ks[11], (H, 4 * H), 0.2), 'lstm_whh1': rn(ks[12], (H, 4 * H), 0.2), 'lstm_b1': jnp.zeros((4 * H,), jnp.float32), 'lstm_wih2': rn(ks[13], (H, 4 * H), 0.2), 'lstm_whh2': rn(ks[14], (H, 4 * H), 0.2), 'lstm_b2': jnp.zeros((4 * H,), jnp.float32)}
    _L0_rec_all = _L0_rec_setup()
    _L0_rec_in = {k: v for k, v in _L0_rec_all.items() if k in ('We', 'Ue', 'be', 'Wx', 'Ws', 'bk', 'enc_w1', 'enc_b1', 'enc_w2', 'enc_b2', 'gate_w', 'gate_b', 'lstm_wih1', 'lstm_whh1', 'lstm_b1', 'lstm_wih2', 'lstm_whh2', 'lstm_b2')}
    del _L0_rec_all
    return {'r_x': r_x, 'r_y': r_y, 'r_error0': r_error0, 'r_gate0': r_gate0, 'L0_rec_We': _L0_rec_in['We'], 'L0_rec_Ue': _L0_rec_in['Ue'], 'L0_rec_be': _L0_rec_in['be'], 'L0_rec_Wx': _L0_rec_in['Wx'], 'L0_rec_Ws': _L0_rec_in['Ws'], 'L0_rec_bk': _L0_rec_in['bk'], 'L0_rec_enc_w1': _L0_rec_in['enc_w1'], 'L0_rec_enc_b1': _L0_rec_in['enc_b1'], 'L0_rec_enc_w2': _L0_rec_in['enc_w2'], 'L0_rec_enc_b2': _L0_rec_in['enc_b2'], 'L0_rec_gate_w': _L0_rec_in['gate_w'], 'L0_rec_gate_b': _L0_rec_in['gate_b'], 'L0_rec_lstm_wih1': _L0_rec_in['lstm_wih1'], 'L0_rec_lstm_whh1': _L0_rec_in['lstm_whh1'], 'L0_rec_lstm_b1': _L0_rec_in['lstm_b1'], 'L0_rec_lstm_wih2': _L0_rec_in['lstm_wih2'], 'L0_rec_lstm_whh2': _L0_rec_in['lstm_whh2'], 'L0_rec_lstm_b2': _L0_rec_in['lstm_b2']}

def reference(r_x, r_y, r_error0, r_gate0, L0_rec_We, L0_rec_Ue, L0_rec_be, L0_rec_Wx, L0_rec_Ws, L0_rec_bk, L0_rec_enc_w1, L0_rec_enc_b1, L0_rec_enc_w2, L0_rec_enc_b2, L0_rec_gate_w, L0_rec_gate_b, L0_rec_lstm_wih1, L0_rec_lstm_whh1, L0_rec_lstm_b1, L0_rec_lstm_wih2, L0_rec_lstm_whh2, L0_rec_lstm_b2):
    import jax
    import jax.numpy as jnp

    def _L0_rec_ref(x, y, error0, gate0, We, Ue, be, Wx, Ws, bk, enc_w1, enc_b1, enc_w2, enc_b2, gate_w, gate_b, lstm_wih1, lstm_whh1, lstm_b1, lstm_wih2, lstm_whh2, lstm_b2):
        import jax, jax.numpy as jnp
        import numpy as np
        MEM, C, S, T_TRAJ, D_IN, H, ENC = (20, 8, 32, 24, 32, 16, 64)
        B, T = (256, 256)

        def _lstm_cell(xt, h, c, wih, whh, b):
            g = xt @ wih + h @ whh + b
            i, f, gg, o = jnp.split(g, 4, axis=1)
            c = jax.nn.sigmoid(f) * c + jax.nn.sigmoid(i) * jnp.tanh(gg)
            h = jax.nn.sigmoid(o) * jnp.tanh(c)
            return (h, c)

        def _clamp01(t):
            return jax.nn.relu(t) - jax.nn.relu(t - 1.0)

        def _forward(x, y, error0, gate0, We, Ue, be, Wx, Ws, bk, enc_w1, enc_b1, enc_w2, enc_b2, gate_w, gate_b, lstm_wih1, lstm_whh1, lstm_b1, lstm_wih2, lstm_whh2, lstm_b2):
            b = x.shape[0]
            mem0 = jnp.zeros((b, MEM, T_TRAJ + 1), x.dtype).at[:, :, -1].set(0.5)
            zS = jnp.zeros((b, S), x.dtype)
            zH = jnp.zeros((b, H), x.dtype)
            carry0 = (zS, error0, gate0, mem0, zH, zH, zH, zH)

            def step(carry, xy):
                xt, yt = xy
                st, err, gs, mem, h1, c1, h2, c2 = carry
                encoded = jnp.tanh(xt @ We + st @ Ue + be)
                new_state = jnp.tanh(jnp.einsum('bd,cds->bcs', xt, Wx) + jnp.einsum('bs,cst->bct', st, Ws) + bk)
                inp = jnp.concatenate([encoded, err[:, None]], axis=1)
                mem = jnp.concatenate([inp[:, None, :], mem[:, :-1, :]], axis=1)
                a = jax.nn.relu(mem.reshape(b, -1) @ enc_w1 + enc_b1)
                agent_in = jax.nn.relu(a @ enc_w2 + enc_b2)
                h1, c1 = _lstm_cell(agent_in, h1, c1, lstm_wih1, lstm_whh1, lstm_b1)
                h2, c2 = _lstm_cell(h1, h2, c2, lstm_wih2, lstm_whh2, lstm_b2)
                gate = jax.nn.softmax(h2 @ gate_w + gate_b, axis=1)
                theta = _clamp01(jnp.mean(jnp.abs(mem[:, :10, -1]), axis=1) * 2.5)[:, None]
                gate = gate * theta + gs * (1.0 - theta)
                st = jnp.einsum('bc,bcs->bs', gate, new_state)
                pred = _clamp01(st[:, -1])
                err = pred - yt
                return ((st, err, gate, mem, h1, c1, h2, c2), pred)
            _, preds = jax.lax.scan(step, carry0, (jnp.swapaxes(x, 0, 1), jnp.swapaxes(y, 0, 1)))
            return jnp.swapaxes(preds, 0, 1)
        return _forward(x, y, error0, gate0, We, Ue, be, Wx, Ws, bk, enc_w1, enc_b1, enc_w2, enc_b2, gate_w, gate_b, lstm_wih1, lstm_whh1, lstm_b1, lstm_wih2, lstm_whh2, lstm_b2)
    y = _L0_rec_ref(r_x, r_y, r_error0, r_gate0, L0_rec_We, L0_rec_Ue, L0_rec_be, L0_rec_Wx, L0_rec_Ws, L0_rec_bk, L0_rec_enc_w1, L0_rec_enc_b1, L0_rec_enc_w2, L0_rec_enc_b2, L0_rec_gate_w, L0_rec_gate_b, L0_rec_lstm_wih1, L0_rec_lstm_whh1, L0_rec_lstm_b1, L0_rec_lstm_wih2, L0_rec_lstm_whh2, L0_rec_lstm_b2)
    return y

_drawn_inputs = setup_inputs


def setup_inputs(seed=0):
    import zlib

    import numpy as np

    out = dict(_drawn_inputs(seed))
    spreads = {'L0_rec_be': (0.0, 2.0),
     'L0_rec_bk': (0.0, 0.1),
     'L0_rec_enc_b1': (0.0, 2.0),
     'L0_rec_enc_b2': (0.0, 2.0),
     'L0_rec_gate_b': (0.0, 0.1),
     'L0_rec_lstm_b1': (0.0, 2.0),
     'L0_rec_lstm_b2': (0.0, 0.1)}
    factors = {'r_y': 8.0,
     'r_error0': 57.372,
     'L0_rec_We': 7.459,
     'L0_rec_Ue': 8.0,
     'L0_rec_enc_w1': 7.445,
     'L0_rec_enc_w2': 4.673,
     'L0_rec_lstm_whh1': 13.785}
    for name, (base, spread) in spreads.items():
        noise = np.random.default_rng([zlib.crc32(name.encode()), seed]).standard_normal(out[name].shape)
        drawn = base * np.exp(spread * noise) if base else spread * noise
        out[name] = jnp.asarray(drawn.astype(out[name].dtype))
    for name, factor in factors.items():
        out[name] = (out[name] * factor).astype(out[name].dtype)
    return out
```

```python
from contextlib import ExitStack

import numpy as np
import concourse.bass as bass
import concourse.mybir as mybir
from concourse.alu_op_type import AluOpType as ALU

FP32, FP16 = mybir.dt.float32, mybir.dt.float16
ACT = mybir.ActivationFunctionType
AX = mybir.AxisListType.X

BATCH, STEPS, D_IN = 2048, 256, 32
MEM, C, S, TRAJ, H, ENC = 20, 8, 32, 24, 16, 64
P = 128
GROUPS = 4
TILES = BATCH // P // GROUPS
GB = TILES * P
INP = TRAJ + 1
NS = C * S
PER_TILE = 5
HT = MEM // PER_TILE
HROWS = PER_TILE * INP
WINDOW = 10
LOOPS = (STEPS - 1) // PER_TILE
FIRST_SLOT = PER_TILE
XROWS = 3 * D_IN + 2
AHEAD_A, AHEAD_B = 3, 2
TABLE = 2 * MEM + 2
assert 1 + LOOPS * PER_TILE == STEPS and HT * PER_TILE == MEM


def recurrent_kernel(nc, x_t, y, error0, gate0, w, ident_c, columns_c, out):
    ctx = ExitStack()
    with ctx:
        def sb(name, shape, dt=FP32):
            return ctx.enter_context(nc.sbuf_tensor(name, shape, dt))

        def sem(name):
            return ctx.enter_context(nc.semaphore(name))

        ident = sb("ident", [P, P])
        ident16 = sb("ident16", [P, P], FP16)
        columns = sb("columns", [P, 4])
        row_scale1, row_scale2, relu_floor, err_rows = (columns[:, c:c + 1] for c in range(4))
        w_x = sb("w_x", [P, NS + TRAJ], FP16)
        w_s = sb("w_s", [P, NS + TRAJ], FP16)
        bias_low = sb("bias_low", [P, NS + TRAJ], FP16)
        enc1_table = sb("enc1_table", [P, TABLE, 2, ENC], FP16)
        now_stage = sb("now_stage", [P, 2, ENC])
        now_parts = sb("now_parts", [P, 2, ENC], FP16)
        w_now = sb("w_now", [P, ENC], FP16)
        w_enc2 = sb("w_enc2", [P, 2, 2 * H])
        enc1_bias = sb("enc1_bias", [P, 1])
        enc2_bias = sb("enc2_bias", [P, 1])
        cell_w = [sb(f"cell_w{n}", [P, TILES, 4 * H]) for n in range(2)]
        gate_w = sb("gate_w", [P, TILES, C])
        CELL_COLS = TILES * 4 * H
        ROW_COLS = 2 * CELL_COLS + TILES * C
        bias_row = sb("bias_row", [1, ROW_COLS])
        bias_parts = sb("bias_parts", [2, ROW_COLS], FP16)
        bias_low_row = sb("bias_low_row", [1, ROW_COLS], FP16)
        ones16 = sb("ones16", [2, P], FP16)
        ones = sb("ones", [P, TILES])

        ys = sb("ys", [P, BATCH // P, STEPS])
        preds = ys
        err_ring = sb("err_ring", [P, BATCH // P, WINDOW])
        x_a = sb("x_a", [AHEAD_A * D_IN, BATCH])
        xh_a = sb("xh_a", [AHEAD_A * D_IN, BATCH], FP16)
        xl_a = sb("xl_a", [AHEAD_A * D_IN, BATCH], FP16)
        x_b = sb("x_b", [AHEAD_B * D_IN, BATCH])
        xh_b = sb("xh_b", [AHEAD_B * D_IN, BATCH], FP16)
        xl_b = sb("xl_b", [AHEAD_B * D_IN, BATCH], FP16)
        xs = sb("xs", [P, PER_TILE + 1, BATCH], FP16)
        hist = sb("hist", [P, 2, HT, BATCH], FP16)
        w_hist = sb("w_hist", [P, PER_TILE + 1, HT, 2, ENC], FP16)

        state_t = sb("state_t", [P, GROUPS, GB], FP16)
        enc = sb("enc", [P, GROUPS, TILES, INP])
        enc_parts = sb("enc_parts", [P, GROUPS, TILES, 4, INP], FP16)
        inp_t = sb("inp_t", [P, GROUPS, GB], FP16)
        a_sb = sb("a_sb", [P, GROUPS, GB // 2])
        zero_h1 = sb("zero_h1", [P, GROUPS, TILES, 2, H])
        h1_h2 = sb("h1_h2", [P, GROUPS, TILES, 2, H])
        cell_in = [sb(f"cell_in{n}", [P, GROUPS, P]) for n in range(2)]
        gate_in = sb("gate_in", [P, GROUPS, P])
        gates = [sb(f"gates{n}", [P, GROUPS, TILES, 4, H]) for n in range(2)]
        keep = [sb(f"keep{n}", [P, GROUPS, TILES, H]) for n in range(2)]
        add = [sb(f"add{n}", [P, GROUPS, TILES, H]) for n in range(2)]
        cell = [sb(f"cell{n}", [P, GROUPS, TILES, H]) for n in range(2)]
        tanh_c = [sb(f"tanh_c{n}", [P, GROUPS, TILES, H]) for n in range(2)]
        cand = sb("cand", [P, GROUPS, TILES, S, C])
        mixed = sb("mixed", [P, 2, TILES, S, C])
        staged = cand[:, :, :, :, :].rearrange("p g j s c -> p (g j s c)")
        x_stage = staged[:, 0:NS + TRAJ]
        s_stage = staged[:, NS + TRAJ:2 * (NS + TRAJ)]
        enc1_stage = staged[:, 2 * (NS + TRAJ):2 * (NS + TRAJ) + MEM * ENC].rearrange("p (m e) -> p m e", e=ENC)
        pred_now = sb("pred_now", [P, GROUPS, TILES])
        state = sb("state", [P, GROUPS, TILES, S])
        state_parts = sb("state_parts", [P, GROUPS, TILES, 4, S], FP16)
        peak = sb("peak", [P, GROUPS, TILES])
        logit = sb("logit", [P, GROUPS, TILES, C])
        expd = sb("expd", [P, GROUPS, TILES, C])
        total = sb("total", [P, GROUPS, TILES])
        share = sb("share", [P, GROUPS, TILES])
        factor = sb("factor", [P, GROUPS, TILES])
        fresh = sb("fresh", [P, GROUPS, TILES, C])
        gate = sb("gate", [P, GROUPS, TILES, C])
        err_sum = sb("err_sum", [P, GROUPS, TILES])
        theta = sb("theta", [P, GROUPS, TILES])
        one_theta = sb("one_theta", [P, GROUPS, TILES])
        kept = sb("kept", [P, GROUPS, TILES, C])

        cand_ps = ctx.enter_context(nc.psum_tensor("cand_ps", [P, TILES * NS], FP32))
        a_ps = [ctx.enter_context(nc.psum_tensor(f"a_ps{n}", [P, 512], FP32)) for n in range(2)]
        chain = [ctx.enter_context(nc.psum_tensor(f"chain{g}", [P, 512], FP32)) for g in range(GROUPS)]

        s_load, s_zero, s_fix, s_prep = sem("s_load"), sem("s_zero"), sem("s_fix"), sem("s_prep")
        s_out = sem("s_out")
        s_xa, s_xb = sem("s_xa_loaded"), sem("s_xb_loaded")
        s_xha, s_xla = sem("s_xa_high"), sem("s_xa_low")
        s_xhb, s_xlb = sem("s_xb_high"), sem("s_xb_low")
        s_xs = [sem(f"s_xs_slot{u}") for u in range(PER_TILE + 1)]
        s_wh = [sem(f"s_w_hist_slot{u}") for u in range(PER_TILE + 1)]
        s_hist = [sem(f"s_hist_group{g}") for g in range(GROUPS)]
        (q_encps, q_enc, q_ench, q_encl, q_inpps, q_inp, q_aps, q_a, q_candps, q_cand) = (
            sem(f"q_{n}") for n in ("encps", "enc", "ench", "encl", "inpps", "inp", "aps", "a",
                                    "candps", "cand"))
        (q_errsum, q_theta, q_onetheta, q_kept, q_pred, q_err, q_errh, q_ring, q_predout) = (
            sem(f"q_{n}") for n in ("errsum", "theta", "onetheta", "kept", "pred", "err", "errh",
                                    "ring", "predout"))
        q_cinps, q_cin, q_cps, q_gates, q_keep, q_add, q_cell, q_tanhc, q_h = (
            [sem(f"q_{n}{c}") for c in range(2)]
            for n in ("cinps", "cin", "cps", "gates", "keep", "add", "cell", "tanhc", "h"))
        q_h1copy = sem("q_h1copy")
        (q_ginps, q_gin, q_logps, q_peak, q_logit, q_exp, q_total, q_share, q_factor, q_fresh,
         q_gate, q_mixv, q_mixp, q_state, q_sh, q_sl, q_stps, q_st) = (
            sem(f"q_{n}") for n in ("ginps", "gin", "logps", "peak", "logit", "exp", "total",
                                    "share", "factor", "fresh", "gate", "mixv", "mixp", "state",
                                    "sh", "sl", "stps", "st"))

        block = ctx.enter_context(nc.Block())

        def over_s(t, g, j):
            n = j.stop - j.start
            return t[:, g, j, :].rearrange("p j (o c) -> p j o c", o=1).to_broadcast([P, n, S, C])

        def slot_of(step_in_turn):
            return FIRST_SLOT if step_in_turn is None else step_in_turn

        def entry_of(step_in_turn):
            return 0 if step_in_turn is None else (1 + step_in_turn) % PER_TILE

        def run_phases(eng, phase, turn_start=None):
            items = []
            for p in range(GROUPS):
                items.insert(0, (p, p + 1, None))
                phase(items[:GROUPS] + [None] * (GROUPS - len(items)), None, None)
            with eng.Fori(0, LOOPS) as turn:
                base = eng.snap(turn * (GROUPS * PER_TILE))
                extra = turn_start(turn) if turn_start else None
                items = [(GROUPS - 1 - q, base + (GROUPS - q), PER_TILE - 1) for q in range(GROUPS)]
                items = [(g, eng.snap(n), u) for g, n, u in items]
                for u in range(PER_TILE):
                    for g in range(GROUPS):
                        n = eng.snap(base + (GROUPS * (u + 1) + g + 1))
                        items = [(g, n, u)] + items[:GROUPS]
                        phase(items[:GROUPS], items[GROUPS], extra)
            items = [(GROUPS - 1 - q, GROUPS * STEPS - q, PER_TILE - 1) for q in range(GROUPS)]
            for p in range(GROUPS - 1):
                items = [None] + items[:GROUPS]
                phase(items[:GROUPS], items[GROUPS], "end")

        @block.sync
        def _(sp):
            loads = [0]

            def load(dst, src):
                sp.dma_start(dst, src).then_inc(s_load, 16)
                loads[0] += 16

            sp.wait_ge(s_zero, 6)
            load(ident[:, :], ident_c)
            load(columns[:, :], columns_c)
            for q in range(4):
                rows = slice(32 * q, 32 * q + 32)
                if q < 3:
                    load(x_stage[rows, 0:NS].rearrange("d (c s) -> d c s", c=C),
                         w["Wx"].rearrange("c d s -> d c s"))
                    load(x_stage[rows, NS:], w["We"])
                load(s_stage[rows, 0:NS].rearrange("d (c s) -> d c s", c=C),
                     w["Ws"].rearrange("c s t -> s c t"))
                load(s_stage[rows, NS:], w["Ue"])
            for r in (96, 97):
                load(x_stage[r:r + 1, 0:NS], w["bk"].rearrange("(o c) s -> o (c s)", o=1))
                load(x_stage[r:r + 1, NS:], w["be"].rearrange("(o a) -> o a", o=1))
            ages = w["enc_w1"].rearrange("(a f) e -> f a e", f=INP)
            for s in range(PER_TILE):
                rows = slice(INP * s, INP * s + INP)
                load(enc1_stage[rows, s + 1:MEM, :], ages[:, 1:MEM - s, :])
                if s:
                    load(enc1_stage[rows, 0:s, :], ages[:, MEM - s:MEM, :])
            for n in range(2):
                load(now_stage[0:INP, n, :], ages[:, 0, :])
            for h in range(2):
                load(w_enc2[ENC * h:ENC * h + ENC, h, 0:H], w["enc_w2"])
                load(enc1_bias[ENC * h:ENC * h + ENC, :], w["enc_b1"].rearrange("(e o) -> e o", o=1))
            for j in range(TILES):
                top, low = slice(32 * j, 32 * j + H), slice(32 * j + H, 32 * j + 2 * H)
                load(enc2_bias[top, :], w["enc_b2"].rearrange("(e o) -> e o", o=1))
                for n in range(2):
                    load(cell_w[n][top, j, :], w[f"lstm_wih{n + 1}"])
                    load(cell_w[n][low, j, :], w[f"lstm_whh{n + 1}"])
                    at = (n * TILES + j) * 4 * H
                    load(bias_row[0:1, at:at + 4 * H],
                         w[f"lstm_b{n + 1}"].rearrange("(o a) -> o a", o=1))
                load(gate_w[low, j, :], w["gate_w"])
                at = 2 * CELL_COLS + C * j
                load(bias_row[0:1, at:at + C], w["gate_b"].rearrange("(o a) -> o a", o=1))
            load(gate[:, :, :, :], gate0.rearrange("(g j p) c -> p g j c", g=GROUPS, p=P))
            load(ys[:, :, :], y.rearrange("(n p) t -> p n t", p=P))
            load(x_b[0:D_IN, :], x_t[0:D_IN, :])
            load(x_a[:, :], x_t[D_IN:D_IN * (1 + AHEAD_A), :])
            with nc.allow_non_contiguous_dma(reason="one error a sequence, once"):
                load(err_ring[:, :, 0:1], error0.rearrange("(n p o) -> p n o", p=P, o=1))
            assert loads[0] == LOADS
            sp.wait_ge(s_prep, PREP_PARTS)
            sp.dma_start(w_x[97:98, :], bias_low[96:97, :]).then_inc(s_fix, 16)
            sp.dma_start(bias_parts[1:2, :], bias_low_row[0:1, :]).then_inc(s_fix, 16)
            for r, part in enumerate((0, 0, 1, 1)):
                sp.dma_start(w_now[INP * r:INP * r + INP, :], now_parts[0:INP, part, :])\
                    .then_inc(s_fix, 16)

            def spread(high, low, row, slot):
                rows = slice(D_IN * row, D_IN * row + D_IN)
                for r, part in enumerate((high, low, high)):
                    sp.dma_start(xs[D_IN * r:D_IN * r + D_IN, slot, :], part[rows, :])\
                        .then_inc(s_xs[slot], 16)

            def history_weights(slot, start):
                sp.dma_start(w_hist[:, slot, :, :, :],
                             enc1_table[:, bass.ds(start, HT, PER_TILE), :, :])\
                    .then_inc(s_wh[slot], 16)

            history_weights(FIRST_SLOT, PER_TILE)
            history_weights(0, PER_TILE + 1)
            sp.wait_ge(s_xlb, 1)
            spread(xh_b, xl_b, 0, FIRST_SLOT)
            sp.dma_start(x_b[:, :], x_t[D_IN * (1 + AHEAD_A):D_IN * (1 + PER_TILE), :])\
                .then_inc(s_xb, 16)
            sp.wait_ge(s_xla, 4)
            for u in range(AHEAD_A):
                spread(xh_a, xl_a, u, u)

            def turn_start(turn):
                here = sp.snap((turn % HT) * BATCH)
                after = sp.snap(((turn + 1) % HT) * BATCH)
                table = sp.snap((turn % HT) * PER_TILE)
                ahead = sp.snap(((turn + 1) % LOOPS) * (PER_TILE * D_IN))
                fours = sp.snap(turn * 4)
                return here, after, table, ahead, fours

            def phase(items, previous, extra):
                new = items[0]
                if new is None:
                    return
                g, n, u = new
                if u is not None:
                    here, after, table, ahead, fours = extra
                    if g == 0:
                        sp.wait_ge(q_candps, items[1][1])
                        sp.wait_ge(q_aps, items[1][1])
                        history_weights((u + 1) % PER_TILE, table + (u + 2 + PER_TILE))
                    if g == 1 and u == 0:
                        sp.wait_ge(s_xlb, fours + 5)
                        for v in range(AHEAD_B):
                            spread(xh_b, xl_b, v, AHEAD_A + v)
                        sp.dma_start(x_a[:, :], x_t[bass.ds(ahead + D_IN, D_IN * AHEAD_A), :])\
                            .then_inc(s_xa, 16)
                    if g == 1 and u == 2:
                        sp.dma_start(x_b[:, :], x_t[bass.ds(ahead + D_IN * (1 + AHEAD_A),
                                                            D_IN * AHEAD_B), :])\
                            .then_inc(s_xb, 16)
                    if g == 1 and u == 3:
                        sp.wait_ge(s_xla, fours + 8)
                        for v in range(AHEAD_A):
                            spread(xh_a, xl_a, v, v)
                rows = slice(INP * entry_of(u), INP * entry_of(u) + INP)
                if u is None:
                    at = GB * g
                else:
                    at = (after if u == PER_TILE - 1 else here) + GB * g
                sp.wait_ge(q_inp, n)
                for part in range(2):
                    dst = hist[rows, part, :, :].rearrange("r k b -> r (k b)")
                    sp.dma_start(dst[:, bass.ds(at, GB)], inp_t[INP * part:INP * part + INP, g, :])\
                        .then_inc(s_hist[g], 16)

            run_phases(sp, phase, turn_start)
            for g in range(GROUPS):
                sp.wait_ge(s_hist[g], 32 * STEPS)
            sp.wait_ge(q_predout, GROUPS * STEPS)
            sp.dma_start(out.rearrange("(n p) t -> p n t", p=P), preds[:, :, :]).then_inc(s_out, 16)
            sp.wait_ge(s_out, 16)

        @block.tensor
        def _(pe):
            pe.wait_ge(s_prep, PREP_ALL)
            pe.wait_ge(s_fix, 16 * 6)

            def parts16(g):
                return chain[g][:, :].bitcast(FP16)

            def cand_or_enc(out_ps, cols, width, data, rows, weights, first):
                for j in range(TILES):
                    last = nc.tensor.matmul(out_ps[:, width * j:width * j + width], data(j),
                                            weights[0:rows, cols], start=first(j), stop=not first(0),
                                            skip_group_check=True)
                return last

            def x_of(slot, g):
                return lambda j: xs[0:XROWS, slot, GB * g + P * j:GB * g + P * j + P]

            def state_of(g):
                return lambda j: state_t[:, g, P * j:P * j + P]

            def encoded(item, previous, x_count):
                g, n, u = item
                if previous is not None:
                    pe.wait_ge(q_st, previous[1])
                if g == 0:
                    pe.wait_ge(s_xs[slot_of(u)], x_count)
                cols = slice(NS, NS + TRAJ)
                cand_or_enc(chain[g], cols, TRAJ, x_of(slot_of(u), g), XROWS, w_x, lambda j: j == 0)
                cand_or_enc(chain[g], cols, TRAJ, state_of(g), P, w_s, lambda j: False)\
                    .then_inc(q_encps, 1)

            def candidates_x(item, before):
                g, n, u = item
                if before is not None:
                    pe.wait_ge(q_cand, before[1])
                cand_or_enc(cand_ps, slice(0, NS), NS, x_of(slot_of(u), g), XROWS, w_x,
                            lambda j: j % 2 == 0)

            def candidates_s(item):
                cand_or_enc(cand_ps, slice(0, NS), NS, state_of(item[0]), P, w_s,
                            lambda j: False).then_inc(q_candps, 1)

            def history(g, slot, kk, waits):
                for s, count in waits:
                    pe.wait_ge(s, count)
                k = HT - 1 - kk
                for t, (wp, xp) in enumerate(((0, 0), (1, 0), (0, 1))):
                    for half in range(2):
                        at = GB * g + 256 * half
                        nc.tensor.matmul(a_ps[g % 2][64 * half:64 * half + ENC, 0:256],
                                         w_hist[0:HROWS, slot, kk, wp, :],
                                         hist[0:HROWS, xp, k, at:at + 256],
                                         start=(kk == 0 and t == 0), stop=False)

            def entry_transposes(item):
                g, n, u = item
                pe.wait_ge(q_encl, n)
                for j in range(TILES):
                    last = nc.tensor.transpose(parts16(g)[0:4 * INP, P * j:P * j + P],
                                               enc_parts[:, g, j, :, :].rearrange("p r f -> p (r f)"),
                                               ident16[:, :])
                last.then_inc(q_inpps, 1)

            def encoder1_now(item, previous):
                g, n, u = item
                pe.wait_ge(q_inp, n)
                for half in range(2):
                    last = nc.tensor.matmul(a_ps[g % 2][64 * half:64 * half + ENC, 0:256],
                                            w_now[0:4 * INP, :],
                                            inp_t[0:4 * INP, g, 256 * half:256 * half + 256],
                                            start=False, stop=True)
                last.then_inc(q_aps, 1)
                if previous is not None:
                    pe.wait_ge(q_h1copy, previous[1])
                nc.tensor.matmul(chain[g][:, 0:P], zero_h1[:, g, :, :, :].rearrange("p j r f -> p (j r f)"),
                                 ident[:, :], is_transpose=True, start=True, stop=True,
                                 skip_group_check=True)

            def encoder2(item):
                g, n, u = item
                pe.wait_ge(q_a, n)
                for j in range(TILES):
                    half, at = j // 2, P * (j % 2)
                    last = nc.tensor.matmul(chain[g][32 * j:32 * j + 32, 0:P],
                                            w_enc2[:, half, :], a_sb[:, g, at:at + P],
                                            start=False, stop=True, skip_group_check=True)
                last.then_inc(q_cinps[0], 1)

            def biased(g, row_at, cols, lhs, rhs, done):
                nc.tensor.matmul(chain[g][:, 0:cols], ones16[0:2, :], bias_parts[0:2, row_at:row_at + cols],
                                 start=True, stop=False, skip_group_check=True)
                nc.tensor.matmul(chain[g][:, 0:cols], lhs, rhs, start=False, stop=True,
                                 skip_group_check=True).then_inc(done, 1)

            def cell_gates(item, c):
                g, n, u = item
                pe.wait_ge(q_cin[c], n)
                biased(g, c * CELL_COLS, CELL_COLS, cell_in[c][:, g, :],
                       cell_w[c][:, :, :].rearrange("p j o -> p (j o)"), q_cps[c])

            def hidden_transpose(item, c, done):
                g, n, u = item
                pe.wait_ge(q_h[c], n)
                nc.tensor.transpose(chain[g][:, 0:P], h1_h2[:, g, :, :, :].rearrange("p j r f -> p (j r f)"),
                                    ident[:, :]).then_inc(done, 1)

            def gate_logits(item):
                g, n, u = item
                pe.wait_ge(q_gin, n)
                biased(g, 2 * CELL_COLS, TILES * C, gate_in[:, g, :],
                       gate_w[:, :, :].rearrange("p j c -> p (j c)"), q_logps)

            def state_transposes(item):
                g, n, u = item
                pe.wait_ge(q_sl, n)
                for j in range(TILES):
                    last = nc.tensor.transpose(parts16(g)[:, P * j:P * j + P],
                                               state_parts[:, g, j, :, :].rearrange("p r f -> p (r f)"),
                                               ident16[:, :])
                last.then_inc(q_stps, 1)

            def turn_start(turn):
                x_count = pe.snap(turn * 48 + 48)
                w_count = pe.snap(turn * 16 + 16)
                w_next = pe.snap(turn * 16 + 32)
                entries = pe.snap(turn * (32 * PER_TILE))
                return x_count, w_count, w_next, entries

            def phase(items, previous, extra):
                q0, q1, q2, q3 = items
                waits = []
                following = None
                if extra is None:
                    x_count = 48
                    g_next = (q0[0] + 1) % GROUPS
                    if g_next == 0:
                        waits = [(s_wh[0], 16), (s_hist[0], 32)]
                    following = (g_next, 0 if g_next == 0 else FIRST_SLOT)
                elif extra != "end":
                    x_count, w_count, w_next, entries = extra
                    g_next, u_next = (q0[0] + 1) % GROUPS, q0[2] + (q0[0] + 1) // GROUPS
                    if g_next == 0:
                        waits = [(s_wh[u_next % PER_TILE], w_next if u_next == PER_TILE else w_count)]
                    waits = waits + [(s_hist[g_next], entries + 32 * (1 + u_next))]
                    following = (g_next, u_next % PER_TILE)
                if following and q1 is not None:
                    waits = waits + [(q_a, q1[1])]
                if q1:
                    encoder2(q1)
                if q2:
                    hidden_transpose(q2, 0, q_cinps[1])
                if q0:
                    encoded(q0, previous, x_count)
                    candidates_x(q0, q1)
                if q1:
                    cell_gates(q1, 0)
                if q0:
                    entry_transposes(q0)
                if q2:
                    cell_gates(q2, 1)
                if q0:
                    candidates_s(q0)
                    encoder1_now(q0, previous)
                if following:
                    history(*following, 0, waits)
                    history(*following, 1, [])
                if q2:
                    hidden_transpose(q2, 1, q_ginps)
                if following:
                    history(*following, 2, [])
                if q2:
                    gate_logits(q2)
                if following:
                    history(*following, 3, [])
                if q3:
                    state_transposes(q3)

            pe.wait_ge(s_wh[FIRST_SLOT], 16)
            for kk in range(HT):
                history(0, FIRST_SLOT, kk, [])
            run_phases(pe, phase, turn_start)

        @block.scalar
        def _(act):
            act.wait_ge(s_prep, PREP_ALL)

            def encoded(item):
                g, n, u = item
                act.wait_ge(q_encps, n)
                src = chain[g][:, 0:TILES * TRAJ].rearrange("p (j f) -> p j f", j=TILES)
                nc.scalar.activation(enc[:, g, :, 0:TRAJ], src, ACT.Tanh).then_inc(q_enc, 1)
                twice = src.rearrange("p j (o f) -> p j o f", o=1).to_broadcast([P, TILES, 2, TRAJ])
                nc.scalar.activation(enc_parts[:, g, :, 0:4:2, 0:TRAJ], twice, ACT.Tanh)\
                    .then_inc(q_ench, 1)

            def entry(item):
                g, n, u = item
                act.wait_ge(q_inpps, n)
                nc.scalar.activation(inp_t[0:4 * INP, g, :], chain[g][:, :].bitcast(FP16)[0:4 * INP, 0:GB],
                                     ACT.Copy).then_inc(q_inp, 1)

            def encoder1(item):
                g, n, u = item
                act.wait_ge(q_aps, n)
                nc.scalar.activation(a_sb[:, g, :], a_ps[g % 2][:, 0:GB // 2], ACT.Relu,
                                     bias=enc1_bias[:, 0:1]).then_inc(q_a, 1)

            def candidates(item):
                g, n, u = item
                act.wait_ge(q_candps, n)
                nc.scalar.activation(cand[:, g, :, :, :].rearrange("p j s c -> p (j s c)"),
                                     cand_ps[:, :], ACT.Tanh).then_inc(q_cand, 1)

            def cell_gates(item, c):
                g, n, u = item
                act.wait_ge(q_cps[c], n)
                nc.scalar.activation(gates[c][:, g, :, :, :].rearrange("p j o h -> p (j o h)"),
                                     chain[g][:, 0:CELL_COLS], ACT.Tanh).then_inc(q_gates[c], 1)

            def cell_tanh(item, c):
                g, n, u = item
                act.wait_ge(q_cell[c], n)
                nc.scalar.activation(tanh_c[c][:, g, :, :], cell[c][:, g, :, :], ACT.Tanh, scale=0.5)\
                    .then_inc(q_tanhc[c], 1)

            def take(item, dst, ready, done):
                g, n, u = item
                act.wait_ge(ready, n)
                nc.scalar.activation(dst[:, g, :], chain[g][:, 0:P], ACT.Copy).then_inc(done, 1)

            def exponentials(item):
                g, n, u = item
                act.wait_ge(q_logit, n)
                nc.scalar.activation(expd[:, g, :, :], logit[:, g, :, :], ACT.Exp).then_inc(q_exp, 1)

            def phase(items, previous, extra):
                q0, q1, q2, q3 = items
                if q2:
                    take(q2, cell_in[1], q_cinps[1], q_cin[1])
                if q0:
                    encoded(q0)
                if q3:
                    exponentials(q3)
                if q1:
                    cell_gates(q1, 0)
                if q0:
                    entry(q0)
                if q2:
                    cell_gates(q2, 1)
                if q1:
                    cell_tanh(q1, 0)
                if q0:
                    encoder1(q0)
                if q2:
                    cell_tanh(q2, 1)
                if q0:
                    candidates(q0)
                if q2:
                    take(q2, gate_in, q_ginps, q_gin)

            run_phases(act, phase)

        @block.vector
        def _(dve):
            V = nc.vector
            V.memset(hist[:, :, :, :].rearrange("p a k b -> p (a k b)").bitcast(FP32), 0.0).then_inc(s_zero, 1)
            V.memset(x_stage[:, :], 0.0).then_inc(s_zero, 1)
            V.memset(enc1_stage[:, :, :], 0.0).then_inc(s_zero, 1)
            for n in range(2):
                V.memset(cell_w[n][:, :, :], 0.0)
            V.memset(gate_w[:, :, :], 0.0)
            V.memset(w_enc2[:, :, :], 0.0)
            V.memset(enc2_bias[:, :], 0.0).then_inc(s_zero, 1)
            V.memset(err_ring[:, :, :], 0.5).then_inc(s_zero, 1)
            V.memset(zero_h1[:, :, :, :, :], 0.0)
            V.memset(h1_h2[:, :, :, :, :], 0.0)
            for n in range(2):
                V.memset(cell[n][:, :, :, :], 0.0)
            V.memset(xs[96:P, :, :], 1.0)
            V.memset(ones16[:, :], 1.0)
            V.memset(ones[:, :], 1.0)
            V.memset(state_t[:, :, :], 0.0).then_inc(s_zero, 1)
            dve.wait_ge(s_zero, 6)
            dve.wait_ge(s_load, LOADS)

            steps = [0]

            def link(ins):
                steps[0] += 1
                ins.then_inc(s_prep, 1)
                dve.wait_ge(s_prep, steps[0])

            def by_source(stage):
                return stage.rearrange("p (c s) -> p s c", c=C)

            def high_parts(high, stage):
                V.tensor_copy(high[:, 0:NS].rearrange("p (s c) -> p s c", c=C), by_source(stage[:, 0:NS]))
                link(V.tensor_copy(high[:, NS:], stage[:, NS:]))

            high_parts(w_s, s_stage)
            high_parts(w_x, x_stage)
            for low, high, stage, rows in ((w_s, w_s, s_stage, slice(64, P)),
                                           (bias_low, w_x, x_stage, slice(96, P)),
                                           (w_x, w_x, x_stage, slice(64, 96))):
                V.tensor_tensor(low[rows, 0:NS].rearrange("p (s c) -> p s c", c=C),
                                by_source(stage[rows, 0:NS]),
                                high[rows, 0:NS].rearrange("p (s c) -> p s c", c=C), ALU.subtract)
                link(V.tensor_tensor(low[rows, NS:], stage[rows, NS:], high[rows, NS:], ALU.subtract))
            for start in range(0, TABLE, MEM):
                m = min(MEM, TABLE - start)
                link(V.tensor_copy(enc1_table[:, start:start + m, 0, :], enc1_stage[:, 0:m, :]))
                link(V.tensor_tensor(enc1_table[:, start:start + m, 1, :], enc1_stage[:, 0:m, :],
                                     enc1_table[:, start:start + m, 0, :], ALU.subtract))
            link(V.tensor_copy(now_parts[0:INP, 0, :], now_stage[0:INP, 0, :]))
            link(V.tensor_tensor(now_parts[0:INP, 1, :], now_stage[0:INP, 0, :],
                                 now_parts[0:INP, 0, :], ALU.subtract))
            for n, scale in enumerate((row_scale1, row_scale2)):
                link(V.tensor_scalar(cell_w[n][:, :, :], cell_w[n][:, :, :], scale, None, ALU.mult))
                link(V.tensor_scalar(cell_w[n][:, :, 0:2 * H], cell_w[n][:, :, 0:2 * H], 0.5, None, ALU.mult))
                link(V.tensor_scalar(cell_w[n][:, :, 3 * H:], cell_w[n][:, :, 3 * H:], 0.5, None, ALU.mult))
            link(V.tensor_scalar(gate_w[:, :, :], gate_w[:, :, :], 0.5, None, ALU.mult))
            rows = bias_row[0:1, 0:2 * CELL_COLS].rearrange("p (j o) -> p j o", o=4 * H)
            link(V.tensor_scalar(rows[:, :, 0:2 * H], rows[:, :, 0:2 * H], 0.5, None, ALU.mult))
            link(V.tensor_scalar(rows[:, :, 3 * H:], rows[:, :, 3 * H:], 0.5, None, ALU.mult))
            link(V.tensor_copy(bias_parts[0:1, :], bias_row[0:1, :]))
            link(V.tensor_tensor(bias_low_row[0:1, :], bias_row[0:1, :], bias_parts[0:1, :], ALU.subtract))
            link(V.tensor_copy(ident16[:, :], ident[:, :]))
            V.tensor_scalar(hist[:, 0, :, :].rearrange("p k b -> p (k b)"),
                            hist[:, 0, :, :].rearrange("p k b -> p (k b)"),
                            err_rows, None, ALU.add).then_inc(s_prep, 1)
            assert steps[0] == PREP_PARTS
            first_error = err_ring[:, :, 0].rearrange("p (g j) -> p g j", g=GROUPS)
            V.tensor_copy(enc[:, :, :, TRAJ], first_error).then_inc(s_prep, 1)
            V.tensor_copy(enc_parts[:, :, :, 0, TRAJ], first_error).then_inc(s_prep, 1)
            V.tensor_copy(enc_parts[:, :, :, 2, TRAJ], first_error).then_inc(s_prep, 1)
            dve.wait_ge(s_prep, PREP_ALL)

            def error_sum(item, before_pool):
                g, n, u = item
                if before_pool is not None:
                    dve.wait_ge(q_ring, before_pool)
                V.tensor_reduce(err_sum[:, g, :], err_ring[:, TILES * g:TILES * g + TILES, :], AX,
                                ALU.add, apply_absolute_value=True).then_inc(q_errsum, 1)

            def thetas(item):
                g, n, u = item
                dve.wait_ge(q_errsum, n)
                V.tensor_scalar(theta[:, g, :], err_sum[:, g, :], 2.5 / WINDOW, 1.0, ALU.mult, ALU.min)\
                    .then_inc(q_theta, 1)

            def entry_low(item, previous):
                g, n, u = item
                dve.wait_ge(q_enc, n)
                dve.wait_ge(q_ench, n)
                if previous is not None:
                    dve.wait_ge(q_errh, previous[1])
                whole = enc[:, g, :, :].rearrange("p j (o f) -> p j o f", o=1)
                V.tensor_tensor(enc_parts[:, g, :, 1:4:2, :], whole.to_broadcast([P, TILES, 2, INP]),
                                enc_parts[:, g, :, 0:1, :].to_broadcast([P, TILES, 2, INP]),
                                ALU.subtract).then_inc(q_encl, 1)

            def cell_input(item):
                g, n, u = item
                dve.wait_ge(q_cinps[0], n)
                V.tensor_scalar(cell_in[0][:, g, :], chain[g][:, 0:P], enc2_bias[:, 0:1], relu_floor,
                                ALU.add, ALU.max).then_inc(q_cin[0], 1)

            def new_cell(item, c):
                g, n, u = item
                gt = gates[c]
                dve.wait_ge(q_gates[c], n)
                V.scalar_tensor_tensor(keep[c][:, g, :, :], gt[:, g, :, 1, :], 1.0, cell[c][:, g, :, :],
                                       ALU.add, ALU.mult).then_inc(q_keep[c], 1)
                V.scalar_tensor_tensor(add[c][:, g, :, :], gt[:, g, :, 0, :], 1.0, gt[:, g, :, 2, :],
                                       ALU.add, ALU.mult).then_inc(q_add[c], 1)
                dve.wait_ge(q_keep[c], n)
                dve.wait_ge(q_add[c], n)
                V.scalar_tensor_tensor(cell[c][:, g, :, :], keep[c][:, g, :, :], 0.5, add[c][:, g, :, :],
                                       ALU.mult, ALU.add).then_inc(q_cell[c], 1)

            def new_hidden(item, c):
                g, n, u = item
                dve.wait_ge(q_tanhc[c], n)
                V.scalar_tensor_tensor(h1_h2[:, g, :, c, :], gates[c][:, g, :, 3, :], 1.0,
                                       tanh_c[c][:, g, :, :], ALU.add, ALU.mult).then_inc(q_h[c], 1)

            def softmax_start(item):
                g, n, u = item
                dve.wait_ge(q_logps, n)
                src = chain[g][:, 0:TILES * C].rearrange("p (j c) -> p j c", c=C)
                V.tensor_reduce(peak[:, g, :], src, AX, ALU.max).then_inc(q_peak, 1)
                dve.wait_ge(q_peak, n)
                V.tensor_tensor(logit[:, g, :, :], src, over_c(peak, g), ALU.subtract).then_inc(q_logit, 1)

            def over_c(t, g):
                return t[:, g, :].rearrange("p (j o) -> p j o", o=1).to_broadcast([P, TILES, C])

            def gate_sum(item):
                g, n, u = item
                dve.wait_ge(q_exp, n)
                V.tensor_reduce(total[:, g, :], expd[:, g, :, :], AX, ALU.add).then_inc(q_total, 1)
                dve.wait_ge(q_total, n)
                V.reciprocal(share[:, g, :], total[:, g, :]).then_inc(q_share, 1)
                dve.wait_ge(q_share, n)
                dve.wait_ge(q_theta, n)
                V.tensor_tensor(factor[:, g, :], share[:, g, :], theta[:, g, :], ALU.mult)\
                    .then_inc(q_factor, 1)
                dve.wait_ge(q_factor, n)
                V.tensor_tensor(fresh[:, g, :, :], expd[:, g, :, :], over_c(factor, g), ALU.mult)\
                    .then_inc(q_fresh, 1)
                dve.wait_ge(q_fresh, n)
                dve.wait_ge(q_kept, n)
                V.tensor_tensor(gate[:, g, :, :], fresh[:, g, :, :], kept[:, g, :, :], ALU.add)\
                    .then_inc(q_gate, 1)

            def mix(item):
                g, n, u = item
                dve.wait_ge(q_gate, n)
                dve.wait_ge(q_cand, n)
                j = slice(0, TILES - 1)
                V.tensor_tensor(mixed[:, g % 2, j, :, :], cand[:, g, j, :, :], over_s(gate, g, j), ALU.mult)\
                    .then_inc(q_mixv, 1)

            def mix_sum(item):
                g, n, u = item
                dve.wait_ge(q_mixv, n)
                dve.wait_ge(q_mixp, n)
                V.tensor_reduce(state[:, g, :, :], mixed[:, g % 2, :, :, :], AX, ALU.add).then_inc(q_state, 1)
                dve.wait_ge(q_state, n)
                twice = state[:, g, :, :].rearrange("p j (o s) -> p j o s", o=1).to_broadcast([P, TILES, 2, S])
                V.tensor_copy(state_parts[:, g, :, 0:4:2, :], twice).then_inc(q_sh, 1)
                V.tensor_scalar(pred_now[:, g, :], state[:, g, :, S - 1], 1.0, 0.0, ALU.min, ALU.max)\
                    .then_inc(q_pred, 1)
                dve.wait_ge(q_sh, n)
                V.tensor_tensor(state_parts[:, g, :, 1:4:2, :], twice,
                                state_parts[:, g, :, 0:1, :].to_broadcast([P, TILES, 2, S]),
                                ALU.subtract).then_inc(q_sl, 1)

            def state_take(item):
                g, n, u = item
                dve.wait_ge(q_stps, n)
                V.tensor_copy(state_t[:, g, :], chain[g][:, :].bitcast(FP16)[:, 0:GB]).then_inc(q_st, 1)

            def phase(items, previous, extra):
                q0, q1, q2, q3 = items
                if q3:
                    softmax_start(q3)
                if q1:
                    cell_input(q1)
                if q0:
                    error_sum(q0, previous[1] if previous else None)
                    thetas(q0)
                if q3:
                    gate_sum(q3)
                if q0:
                    entry_low(q0, previous)
                if q1:
                    new_cell(q1, 0)
                if q3:
                    mix(q3)
                if q2:
                    new_cell(q2, 1)
                if q1:
                    new_hidden(q1, 0)
                if q2:
                    new_hidden(q2, 1)
                if q3:
                    mix_sum(q3)
                    state_take(q3)

            run_phases(dve, phase)

        @block.gpsimd
        def _(pool):
            G = nc.gpsimd
            pool.wait_ge(s_load, LOADS)
            G.tensor_copy(xh_b[0:D_IN, :], x_b[0:D_IN, :]).then_inc(s_xhb, 1)
            pool.wait_ge(s_xhb, 1)
            G.tensor_tensor(xl_b[0:D_IN, :], x_b[0:D_IN, :], xh_b[0:D_IN, :], ALU.subtract).then_inc(s_xlb, 1)

            def x_high(dst, src, k, done):
                G.tensor_copy(dst[:, 512 * k:512 * k + 512], src[:, 512 * k:512 * k + 512]).then_inc(done, 1)

            def x_low(dst, src, high, k, done):
                cols = slice(512 * k, 512 * k + 512)
                G.tensor_tensor(dst[:, cols], src[:, cols], high[:, cols], ALU.subtract).then_inc(done, 1)

            for k in range(4):
                x_high(xh_a, x_a, k, s_xha)
            for k in range(4):
                pool.wait_ge(s_xha, k + 1)
                x_low(xl_a, x_a, xh_a, k, s_xla)
            pool.wait_ge(s_xb, 16)
            pool.wait_ge(s_xs[FIRST_SLOT], 48)
            for k in range(4):
                x_high(xh_b, x_b, k, s_xhb)
            for k in range(4):
                pool.wait_ge(s_xhb, k + 2)
                x_low(xl_b, x_b, xh_b, k, s_xlb)
            pool.wait_ge(s_prep, PREP_ALL)

            def thetas(item):
                g, n, u = item
                pool.wait_ge(q_theta, n)
                G.tensor_tensor(one_theta[:, g, :], ones[:, :], theta[:, g, :], ALU.subtract)\
                    .then_inc(q_onetheta, 1)
                pool.wait_ge(q_onetheta, n)
                G.tensor_tensor(kept[:, g, :, :], gate[:, g, :, :],
                                one_theta[:, g, :].rearrange("p (j o) -> p j o", o=1)
                                .to_broadcast([P, TILES, C]), ALU.mult).then_inc(q_kept, 1)

            def copy_h1(item):
                g, n, u = item
                pool.wait_ge(q_h[0], n)
                every = ones[:, :].rearrange("p (j o) -> p j o", o=1).to_broadcast([P, TILES, H])
                G.tensor_tensor(zero_h1[:, g, :, 1, :], h1_h2[:, g, :, 0, :], every, ALU.mult)\
                    .then_inc(q_h1copy, 1)

            def mix(item):
                g, n, u = item
                pool.wait_ge(q_gate, n)
                pool.wait_ge(q_cand, n)
                j = slice(TILES - 1, TILES)
                G.tensor_tensor(mixed[:, g % 2, j, :, :], cand[:, g, j, :, :], over_s(gate, g, j), ALU.mult)\
                    .then_inc(q_mixp, 1)

            def predict(item, step, ring):
                g, n, u = item
                tiles = slice(TILES * g, TILES * g + TILES)
                pred = pred_now[:, g, :].rearrange("p (j o) -> p j o", o=1)
                pool.wait_ge(q_pred, n)
                G.tensor_tensor(enc[:, g, :, TRAJ:INP], pred, ys[:, tiles, bass.ds(step, 1)], ALU.subtract)\
                    .then_inc(q_err, 1)
                pool.wait_ge(q_err, n)
                twice = enc[:, g, :, TRAJ:INP].to_broadcast([P, TILES, 2])
                every = ones[:, :].rearrange("p (j o) -> p j o", o=1).to_broadcast([P, TILES, 2])
                G.tensor_tensor(enc_parts[:, g, :, 0:4:2, TRAJ], twice, every, ALU.mult).then_inc(q_errh, 1)
                G.tensor_copy(preds[:, tiles, bass.ds(step, 1)], pred).then_inc(q_predout, 1)
                G.tensor_copy(err_ring[:, tiles, bass.ds(ring, 1)], enc[:, g, :, TRAJ:INP])\
                    .then_inc(q_ring, 1)

            def turn_start(turn):
                step = pool.snap(turn * PER_TILE)
                odd = pool.snap((turn % 2) * PER_TILE)
                even = pool.snap((turn + 1) % 2 * PER_TILE)
                loaded = pool.snap(turn * 16 + 16)
                fours = pool.snap(turn * 4)
                spreads = pool.snap(turn * 48 + 48)
                return step, odd, even, loaded, fours, spreads

            def x_waits(u, k, extra):
                step, odd, even, loaded, fours, spreads = extra
                if u == 1 and k == 0:
                    pool.wait_ge(s_xa, loaded)
                    for v in range(AHEAD_A):
                        pool.wait_ge(s_xs[v], spreads)
                elif u == 3 and k == 0:
                    pool.wait_ge(s_xb, loaded + 16)
                    for v in range(AHEAD_B):
                        pool.wait_ge(s_xs[AHEAD_A + v], spreads)

            def x_parts(u, k, extra):
                step, odd, even, loaded, fours, spreads = extra
                if u == 1:
                    x_high(xh_a, x_a, k, s_xha)
                elif u == 2:
                    pool.wait_ge(s_xha, fours + (k + 5))
                    x_low(xl_a, x_a, xh_a, k, s_xla)
                elif u == 3:
                    x_high(xh_b, x_b, k, s_xhb)
                elif u == 4:
                    pool.wait_ge(s_xhb, fours + (k + 6))
                    x_low(xl_b, x_b, xh_b, k, s_xlb)

            def phase(items, previous, extra):
                q0, q1, q2, q3 = items
                if q0 and q0[2] is not None:
                    x_waits(q0[2], q0[0], extra)
                if q0:
                    thetas(q0)
                if q0 and q0[2] is not None:
                    x_parts(q0[2], q0[0], extra)
                if q3:
                    mix(q3)
                if q1:
                    copy_h1(q1)
                if q3:
                    g, n, u = q3
                    if extra is None:
                        predict(q3, 0, 1)
                    elif extra == "end":
                        predict(q3, STEPS - 1, STEPS % WINDOW)
                    else:
                        step, odd, even = extra[:3]
                        v = q0[2] - (q0[0] != GROUPS - 1)
                        place = v + 2
                        ring = odd + place if place < PER_TILE else even + (place - PER_TILE)
                        predict(q3, step + (v + 1), ring)

            run_phases(pool, phase, turn_start)


LOADS = 16 * (2 + 3 * 2 + 4 * 2 + 2 * 2 + (2 * PER_TILE - 1) + 2 + 4 + TILES * (1 + 2 * 3 + 2) + 5)
PREP_PARTS = 2 + 3 + 2 * 3 + 2 + 6 + 1 + 2 + 2 + 1
PREP_ALL = PREP_PARTS + 4

WEIGHTS = ("We", "Ue", "be", "Wx", "Ws", "bk", "enc_w1", "enc_b1", "enc_w2", "enc_b2", "gate_w",
           "gate_b", "lstm_wih1", "lstm_whh1", "lstm_b1", "lstm_wih2", "lstm_whh2", "lstm_b2")


def kernel(**inputs):
    import concourse.bacc as bacc
    from concourse.bass_utils import run_bass_kernel_spmd

    nc = bacc.Bacc("TRN2", target_bir_lowering=False, num_devices=1)
    arrays = {}

    def give(name, a):
        a = np.ascontiguousarray(a)
        arrays["in_" + name] = a
        return nc.dram_tensor("in_" + name, a.shape, mybir.dt.from_np(a.dtype), kind="ExternalInput").ap()

    x = np.asarray(inputs["r_x"])
    x_t = give("x_t", np.transpose(x, (1, 2, 0)).reshape(STEPS * D_IN, BATCH))
    y = give("y", inputs["r_y"])
    error0 = give("error0", inputs["r_error0"])
    gate0 = give("gate0", inputs["r_gate0"])
    w = {n: give(n, inputs[f"L0_rec_{n}"]) for n in WEIGHTS}
    row = np.arange(P)
    columns = np.zeros((P, 4), np.float32)
    columns[:, 0] = np.where(row % 32 < H, 1.0, 0.5)
    columns[:, 1] = 0.5
    columns[:, 2] = np.where(row % 32 < H, 0.0, -3.0e38)
    columns[:, 3] = np.where((row % INP == INP - 1) & (row < HROWS), 0.5, 0.0)
    ident_c = give("ident_c", np.eye(P, dtype=np.float32))
    columns_c = give("columns_c", columns)
    out = nc.dram_tensor("preds_out", (BATCH, STEPS), FP32, kind="ExternalOutput").ap()
    recurrent_kernel(nc, x_t, y, error0, gate0, w, ident_c, columns_c, out)
    result = run_bass_kernel_spmd(nc, [arrays], core_ids=[0])
    return result.results[0]["preds_out"]
```

```python
from contextlib import ExitStack

import numpy as np
import concourse.bass as bass
import concourse.mybir as mybir
from concourse.alu_op_type import AluOpType as ALU

FP32, FP16 = mybir.dt.float32, mybir.dt.float16
ACT = mybir.ActivationFunctionType
AX = mybir.AxisListType.X

BATCH, STEPS, D_IN = 2048, 256, 32
MEM, C, S, TRAJ, H, ENC = 20, 8, 32, 24, 16, 64
P = 128
GROUPS = 4
TILES = BATCH // P // GROUPS
GB = TILES * P
INP = TRAJ + 1
NS = C * S
PER_TILE = 5
HT = MEM // PER_TILE
HROWS = PER_TILE * INP
WINDOW = 10
LOOPS = (STEPS - 1) // PER_TILE
FIRST_SLOT = PER_TILE - 1
DEPTH = 5
XROWS = 3 * D_IN + 2
AHEAD_A, AHEAD_B = 3, 2
TABLE = 2 * MEM + 2
PARTS = 3
OUT_AT = 256
CELL_IN = TILES * H
MIX_V = 2
assert 1 + LOOPS * PER_TILE == STEPS and HT * PER_TILE == MEM


def recurrent_kernel(nc, x_t, y, error0, gate0, w, ident_c, columns_c, out):
    ctx = ExitStack()
    with ctx:
        def sb(name, shape, dt=FP32):
            return ctx.enter_context(nc.sbuf_tensor(name, shape, dt))

        def sem(name):
            return ctx.enter_context(nc.semaphore(name))

        ident = sb("ident", [P, P])
        ident16 = sb("ident16", [P, P], FP16)
        columns = sb("columns", [P, 2])
        row_scale0, err_rows = (columns[:, c:c + 1] for c in range(2))
        w_x = sb("w_x", [P, NS + TRAJ], FP16)
        w_s = sb("w_s", [P, NS + TRAJ], FP16)
        bias_low = sb("bias_low", [P, NS + TRAJ], FP16)
        enc1_table = sb("enc1_table", [P, TABLE, 2, ENC], FP16)
        now_stage = sb("now_stage", [P, 2, ENC])
        now_parts = sb("now_parts", [P, 2, ENC], FP16)
        w_now = sb("w_now", [P, ENC], FP16)
        w_enc2 = sb("w_enc2", [P, 2 * H])
        enc1_bias = sb("enc1_bias", [P, 1])
        enc2_bias = sb("enc2_bias", [CELL_IN, 1])
        cell_w = [sb(f"cell_w{n}", [P, TILES, 4 * H]) for n in range(2)]
        gate_w = sb("gate_w", [CELL_IN, TILES, C])
        CELL_COLS = TILES * 4 * H
        ROW_COLS = 2 * CELL_COLS + TILES * C
        bias_row = sb("bias_row", [1, ROW_COLS])
        bias_parts = sb("bias_parts", [2, ROW_COLS], FP16)
        bias_low_row = sb("bias_low_row", [1, ROW_COLS], FP16)
        ones16 = sb("ones16", [2, P], FP16)
        ones = sb("ones", [P, TILES])

        ys = sb("ys", [P, BATCH // P, STEPS])
        preds = ys
        err_ring = sb("err_ring", [P, BATCH // P, WINDOW])
        x_a = sb("x_a", [AHEAD_A * D_IN, BATCH])
        xh_a = sb("xh_a", [AHEAD_A * D_IN, BATCH], FP16)
        xl_a = sb("xl_a", [AHEAD_A * D_IN, BATCH], FP16)
        x_b = sb("x_b", [AHEAD_B * D_IN, BATCH])
        xh_b = sb("xh_b", [AHEAD_B * D_IN, BATCH], FP16)
        xl_b = sb("xl_b", [AHEAD_B * D_IN, BATCH], FP16)
        xs = sb("xs", [P, PER_TILE, BATCH], FP16)
        hist = sb("hist", [P, 2, HT, BATCH], FP16)
        w_hist = sb("w_hist", [P, PER_TILE, HT, 2, ENC], FP16)

        state_t = sb("state_t", [P, GROUPS, GB], FP16)
        enc = sb("enc", [P, GROUPS, TILES, INP])
        enc_parts = sb("enc_parts", [P, GROUPS, TILES, PARTS, INP], FP16)
        inp_t = sb("inp_t", [P, GROUPS, GB], FP16)
        a_sb = sb("a_sb", [P, GROUPS, GB // 2])
        h_both = sb("h_both", [P, GROUPS, 2, TILES, H])
        h = [h_both[:, :, 1 - n, :, :] for n in range(2)]
        cell_in = [sb(f"cell_in{n}", [P, GROUPS, P]) for n in range(2)]
        gates = [sb(f"gates{n}", [P, GROUPS, TILES, 5, H]) for n in range(2)]
        added = [sb(f"added{n}", [P, GROUPS, TILES, 2, H]) for n in range(2)]
        tanh_c = [sb(f"tanh_c{n}", [P, GROUPS, TILES, H]) for n in range(2)]
        cand = sb("cand", [P, GROUPS, TILES, S, C])
        mixed = sb("mixed", [P, 2, TILES, S, C])
        staged = cand[:, :, :, :, :].rearrange("p g j s c -> p (g j s c)")
        x_stage = staged[:, 0:NS + TRAJ]
        s_stage = staged[:, NS + TRAJ:2 * (NS + TRAJ)]
        enc1_stage = staged[:, 2 * (NS + TRAJ):2 * (NS + TRAJ) + MEM * ENC].rearrange("p (m e) -> p m e", e=ENC)
        pred_now = sb("pred_now", [P, GROUPS, TILES])
        state = sb("state", [P, GROUPS, TILES, S])
        state_parts = sb("state_parts", [P, GROUPS, TILES, PARTS, S], FP16)
        peak = sb("peak", [P, GROUPS, TILES])
        logit = sb("logit", [P, GROUPS, TILES, C])
        expd = sb("expd", [P, GROUPS, TILES, C])
        total = sb("total", [P, GROUPS, TILES])
        share = sb("share", [P, GROUPS, TILES])
        weighted = sb("weighted", [P, GROUPS, TILES, C])
        fresh = sb("fresh", [P, GROUPS, TILES, C])
        gate = sb("gate", [P, GROUPS, TILES, C])
        err_sum = sb("err_sum", [P, GROUPS, TILES])
        theta = sb("theta", [P, GROUPS, TILES])
        one_theta = sb("one_theta", [P, GROUPS, TILES])
        kept = sb("kept", [P, GROUPS, TILES, C])

        cand_ps = ctx.enter_context(nc.psum_tensor("cand_ps", [P, TILES * NS], FP32))
        a_ps = [ctx.enter_context(nc.psum_tensor(f"a_ps{n}", [P, 512], FP32)) for n in range(2)]
        chain = [ctx.enter_context(nc.psum_tensor(f"chain{g}", [P, 512], FP32)) for g in range(GROUPS)]

        s_load, s_zero, s_fix, s_prep = sem("s_load"), sem("s_zero"), sem("s_fix"), sem("s_prep")
        s_out = sem("s_out")
        s_xa, s_xb = sem("s_xa_loaded"), sem("s_xb_loaded")
        s_xha, s_xla = sem("s_xa_high"), sem("s_xa_low")
        s_xhb, s_xlb = sem("s_xb_high"), sem("s_xb_low")
        s_xs = [sem(f"s_xs_slot{u}") for u in range(PER_TILE)]
        s_wh = [sem(f"s_w_hist_slot{u}") for u in range(PER_TILE)]
        s_hist = [sem(f"s_hist_group{g}") for g in range(GROUPS)]
        (q_encps, q_enc, q_encl, q_inpps, q_inp, q_aps, q_a, q_candps, q_cand) = (
            sem(f"q_{n}") for n in ("encps", "enc", "encl", "inpps", "inp", "aps", "a",
                                    "candps", "cand"))
        (q_errsum, q_theta, q_onetheta, q_kept, q_pred, q_err, q_errh, q_ring, q_predout) = (
            sem(f"q_{n}") for n in ("errsum", "theta", "onetheta", "kept", "pred", "err", "errh",
                                    "ring", "predout"))
        q_cps, q_gates, q_added, q_cell, q_tanhc, q_h, q_hps, q_ht = (
            [sem(f"q_{n}{c}") for c in range(2)]
            for n in ("cps", "gates", "added", "cell", "tanhc", "h", "hps", "ht"))
        (q_cinps, q_cin, q_hnext, q_logps, q_peak, q_logit, q_exp, q_total, q_share, q_fresh,
         q_gate, q_mixv, q_mixp, q_sumv, q_sump, q_sh, q_sl, q_stps, q_st) = (
            sem(f"q_{n}") for n in ("cinps", "cin", "hnext", "logps", "peak", "logit", "exp",
                                    "total", "share", "fresh", "gate", "mixv", "mixp", "sumv",
                                    "sump", "sh", "sl", "stps", "st"))

        block = ctx.enter_context(nc.Block())

        def over_s(t, g, j):
            n = j.stop - j.start
            return t[:, g, j, :].rearrange("p j (o c) -> p j o c", o=1).to_broadcast([P, n, S, C])

        def slot_of(u):
            return u % PER_TILE

        def entry_of(u):
            return (1 + u) % PER_TILE

        def run_phases(eng, phase, turn_start=None):
            items = [None] * DEPTH
            for p in range(GROUPS):
                items = [(p, p + 1, -1)] + items[:DEPTH - 1]
                phase(items, None)
            with eng.Fori(0, LOOPS) as turn:
                base = eng.snap(turn * (GROUPS * PER_TILE))
                extra = turn_start(turn) if turn_start else None
                items = [(g, eng.snap(base + (g + 1)), -1) for g in reversed(range(GROUPS))]
                for u in range(PER_TILE):
                    for g in range(GROUPS):
                        n = eng.snap(base + (GROUPS * (u + 1) + g + 1))
                        items = [(g, n, u)] + items[:DEPTH - 1]
                        phase(items, extra)
            items = [(g, GROUPS * (STEPS - 1) + g + 1, -1) for g in reversed(range(GROUPS))]
            for p in range(DEPTH - 1):
                items = [None] + items[:DEPTH - 1]
                phase(items, "end")

        def load_by(eng):
            def load(dst, src):
                eng.dma_start(dst, src).then_inc(s_load, 16)
                loads[0] += 16
            return load

        loads = [0]

        @block.sync
        def _(sp):
            load = load_by(sp)
            load(ident[:, :], ident_c)
            load(columns[:, :], columns_c)
            load(gate[:, :, :, :], gate0.rearrange("(g j p) c -> p g j c", g=GROUPS, p=P))
            load(x_b[0:D_IN, :], x_t[0:D_IN, :])
            load(x_a[:, :], x_t[D_IN:D_IN * (1 + AHEAD_A), :])
            load(ys[:, :, :], y.rearrange("(n p) t -> p n t", p=P))
            sp.wait_ge(s_zero, ZEROED)
            for q in range(PARTS):
                rows = slice(32 * q, 32 * q + 32)
                load(x_stage[rows, 0:NS].rearrange("d (c s) -> d c s", c=C),
                     w["Wx"].rearrange("c d s -> d c s"))
                load(x_stage[rows, NS:], w["We"])
                load(s_stage[rows, 0:NS].rearrange("d (c s) -> d c s", c=C),
                     w["Ws"].rearrange("c s t -> s c t"))
                load(s_stage[rows, NS:], w["Ue"])
            for r in (96, 97):
                load(x_stage[r:r + 1, 0:NS], w["bk"].rearrange("(o c) s -> o (c s)", o=1))
                load(x_stage[r:r + 1, NS:], w["be"].rearrange("(o a) -> o a", o=1))
            ages = w["enc_w1"].rearrange("(a f) e -> f a e", f=INP)
            for s in range(PER_TILE):
                rows = slice(INP * s, INP * s + INP)
                load(enc1_stage[rows, s + 1:MEM, :], ages[:, 1:MEM - s, :])
                if s:
                    load(enc1_stage[rows, 0:s, :], ages[:, MEM - s:MEM, :])
            for n in range(2):
                load(now_stage[0:INP, n, :], ages[:, 0, :])
            for half in range(2):
                rows = slice(ENC * half, ENC * half + ENC)
                load(w_enc2[rows, H * half:H * half + H], w["enc_w2"])
                load(enc1_bias[rows, :], w["enc_b1"].rearrange("(e o) -> e o", o=1))

            with nc.allow_non_contiguous_dma(reason="one error a sequence, once"):
                load(err_ring[:, :, 0:1], error0.rearrange("(n p o) -> p n o", p=P, o=1))
            sp.wait_ge(s_prep, PREP_PARTS)
            sp.dma_start(w_x[97:98, :], bias_low[96:97, :]).then_inc(s_fix, 16)
            sp.dma_start(bias_parts[1:2, :], bias_low_row[0:1, :]).then_inc(s_fix, 16)
            for r, part in enumerate((0, 0, 1)):
                sp.dma_start(w_now[INP * r:INP * r + INP, :], now_parts[0:INP, part, :])\
                    .then_inc(s_fix, 16)

            def spread(high, low, row, slot):
                rows = slice(D_IN * row, D_IN * row + D_IN)
                for r, part in enumerate((high, low, high)):
                    sp.dma_start(xs[D_IN * r:D_IN * r + D_IN, slot, :], part[rows, :])\
                        .then_inc(s_xs[slot], 16)

            def history_weights(slot, start):
                sp.dma_start(w_hist[:, slot, :, :, :],
                             enc1_table[:, bass.ds(start, HT, PER_TILE), :, :])\
                    .then_inc(s_wh[slot], 16)

            history_weights(FIRST_SLOT, PER_TILE)
            history_weights(0, PER_TILE + 1)
            sp.wait_ge(s_xlb, 1)
            spread(xh_b, xl_b, 0, FIRST_SLOT)
            sp.dma_start(x_b[:, :], x_t[D_IN * (1 + AHEAD_A):D_IN * (1 + PER_TILE), :])\
                .then_inc(s_xb, 16)
            sp.wait_ge(s_xla, 4)
            for u in range(AHEAD_A):
                spread(xh_a, xl_a, u, u)

            def turn_start(turn):
                here = sp.snap((turn % HT) * BATCH)
                after = sp.snap(((turn + 1) % HT) * BATCH)
                table = sp.snap((turn % HT) * PER_TILE)
                ahead = sp.snap(((turn + 1) % LOOPS) * (PER_TILE * D_IN))
                fours = sp.snap(turn * 4)
                return here, after, table, ahead, fours

            def phase(items, extra):
                if items[0] is None:
                    return
                g, n, u = items[0]
                if extra is not None:
                    here, after, table, ahead, fours = extra
                    if g == 0:
                        sp.wait_ge(q_candps, items[1][1])
                        sp.wait_ge(q_aps, items[1][1])
                        history_weights((u + 1) % PER_TILE, table + (u + 2 + PER_TILE))
                    if g == 1 and u == 0:
                        sp.wait_ge(s_xlb, fours + 5)
                        for v in range(AHEAD_B):
                            spread(xh_b, xl_b, v, AHEAD_A + v)
                        sp.dma_start(x_a[:, :], x_t[bass.ds(ahead + D_IN, D_IN * AHEAD_A), :])\
                            .then_inc(s_xa, 16)
                    if g == 1 and u == 2:
                        sp.dma_start(x_b[:, :], x_t[bass.ds(ahead + D_IN * (1 + AHEAD_A),
                                                            D_IN * AHEAD_B), :])\
                            .then_inc(s_xb, 16)
                    if g == 1 and u == 3:
                        sp.wait_ge(s_xla, fours + 8)
                        for v in range(AHEAD_A):
                            spread(xh_a, xl_a, v, v)
                rows = slice(INP * entry_of(u), INP * entry_of(u) + INP)
                if extra is None:
                    at = GB * g
                else:
                    at = (after if u == PER_TILE - 1 else here) + GB * g
                sp.wait_ge(q_aps, n)
                sp.wait_ge(q_inp, n)
                for part in range(2):
                    dst = hist[rows, part, :, :].rearrange("r k b -> r (k b)")
                    sp.dma_start(dst[:, bass.ds(at, GB)], inp_t[INP * part:INP * part + INP, g, :])\
                        .then_inc(s_hist[g], 16)

            run_phases(sp, phase, turn_start)
            for g in range(GROUPS):
                sp.wait_ge(s_hist[g], 32 * STEPS)
            sp.wait_ge(q_predout, GROUPS * STEPS)
            sp.dma_start(out.rearrange("(n p) t -> p n t", p=P), preds[:, :, :]).then_inc(s_out, 16)
            sp.wait_ge(s_out, 16)

        @block.tensor
        def _(pe):
            pe.wait_ge(s_prep, PREP_ALL)
            pe.wait_ge(s_fix, 16 * 5)

            def parts16(g):
                return chain[g][:, :].bitcast(FP16)

            def cand_or_enc(out_ps, cols, width, data, rows, weights, first):
                for j in range(TILES):
                    last = nc.tensor.matmul(out_ps[:, width * j:width * j + width], data(j),
                                            weights[0:rows, cols], start=first(j), stop=not first(0),
                                            skip_group_check=True)
                return last

            def x_of(slot, g):
                return lambda j: xs[0:XROWS, slot, GB * g + P * j:GB * g + P * j + P]

            def state_of(g):
                return lambda j: state_t[0:PARTS * S, g, P * j:P * j + P]

            def x_wait(item, extra):
                g, n, u = item
                if g == 0:
                    pe.wait_ge(s_xs[slot_of(u)], extra[0][u] if extra else 48)

            def encoded(item, extra):
                g, n, u = item
                pe.wait_ge(q_st, n)
                x_wait(item, extra)
                cols = slice(NS, NS + TRAJ)
                cand_or_enc(chain[g], cols, TRAJ, x_of(slot_of(u), g), XROWS, w_x, lambda j: j == 0)
                cand_or_enc(chain[g], cols, TRAJ, state_of(g), PARTS * S, w_s, lambda j: False)\
                    .then_inc(q_encps, 1)

            def candidates_x(item, before, extra):
                g, n, u = item
                if before:
                    pe.wait_ge(q_cand, before[1])
                x_wait(item, extra)
                cand_or_enc(cand_ps, slice(0, NS), NS, x_of(slot_of(u), g), XROWS, w_x,
                            lambda j: j % 2 == 0)

            def candidates_s(item):
                g, n, u = item
                pe.wait_ge(q_st, n)
                cand_or_enc(cand_ps, slice(0, NS), NS, state_of(g), PARTS * S, w_s,
                            lambda j: False).then_inc(q_candps, 1)

            def history_waits(item, before, extra):
                g, n, u = item
                if g == 0:
                    pe.wait_ge(s_wh[slot_of(u)], extra[1][u] if extra else 16)
                if extra:
                    pe.wait_ge(s_hist[g], extra[2][u])
                if before:
                    pe.wait_ge(q_a, before[1])

            def history(item, kk):
                g, n, u = item
                k = HT - 1 - kk
                for t, (wp, xp) in enumerate(((0, 0), (1, 0), (0, 1))):
                    for half in range(2):
                        at = GB * g + 256 * half
                        nc.tensor.matmul(a_ps[g % 2][64 * half:64 * half + ENC, 0:256],
                                         w_hist[0:HROWS, slot_of(u), kk, wp, :],
                                         hist[0:HROWS, xp, k, at:at + 256],
                                         start=(kk == 0 and t == 0), stop=False)

            def entry_transposes(item):
                g, n, u = item
                pe.wait_ge(q_encl, n)
                for j in range(TILES):
                    last = nc.tensor.transpose(parts16(g)[0:PARTS * INP, P * j:P * j + P],
                                               enc_parts[:, g, j, :, :].rearrange("p r f -> p (r f)"),
                                               ident16[:, :])
                last.then_inc(q_inpps, 1)

            def encoder1_now(item):
                g, n, u = item
                pe.wait_ge(q_inp, n)
                for half in range(2):
                    last = nc.tensor.matmul(a_ps[g % 2][64 * half:64 * half + ENC, 0:256],
                                            w_now[0:PARTS * INP, :],
                                            inp_t[0:PARTS * INP, g, 256 * half:256 * half + 256],
                                            start=False, stop=True)
                last.then_inc(q_aps, 1)

            def encoder2(item):
                g, n, u = item
                pe.wait_ge(q_a, n)
                for m in range(2):
                    last = nc.tensor.matmul(chain[g][32 * m:32 * m + 32, 0:P], w_enc2[:, :],
                                            a_sb[:, g, P * m:P * m + P], start=False, stop=True,
                                            skip_group_check=True)
                last.then_inc(q_cinps, 1)

            def bias(item, row_at, cols, free, count):
                g, n, u = item
                pe.wait_ge(free, count)
                nc.tensor.matmul(chain[g][:, OUT_AT:OUT_AT + cols], ones16[0:2, :],
                                 bias_parts[0:2, row_at:row_at + cols],
                                 start=True, stop=False, skip_group_check=True)

            def cell_bias(item, c):
                bias(item, c * CELL_COLS, CELL_COLS, (q_inp, q_gates[0])[c], item[1])

            def logit_bias(item):
                bias(item, 2 * CELL_COLS, TILES * C, q_gates[1], item[1])

            def cell_gates(item, c):
                g, n, u = item
                pe.wait_ge((q_cin, q_ht[0])[c], n)
                nc.tensor.matmul(chain[g][:, OUT_AT:OUT_AT + CELL_COLS], cell_in[c][:, g, :],
                                 cell_w[c][:, :, :].rearrange("p j o -> p (j o)"), start=False,
                                 stop=True, skip_group_check=True).then_inc(q_cps[c], 1)

            def hidden_transpose(item, c):
                g, n, u = item
                pe.wait_ge(q_h[c], n)
                nc.tensor.matmul(chain[g][:, 0:P], h_both[:, g, :, :, :].rearrange("p n j f -> p (n j f)"),
                                 ident[:, :], is_transpose=True, start=False, stop=True,
                                 skip_group_check=True).then_inc(q_hps[c], 1)

            def gate_logits(item):
                g, n, u = item
                pe.wait_ge(q_ht[1], n + GROUPS)
                nc.tensor.matmul(chain[g][:, OUT_AT:OUT_AT + TILES * C], cell_in[1][0:CELL_IN, g, :],
                                 gate_w[:, :, :].rearrange("p j c -> p (j c)"), start=False,
                                 stop=True, skip_group_check=True).then_inc(q_logps, 1)

            def state_transposes(item):
                g, n, u = item
                pe.wait_ge(q_sl, n)
                for j in range(TILES):
                    last = nc.tensor.transpose(parts16(g)[0:PARTS * S, P * j:P * j + P],
                                               state_parts[:, g, j, :, :].rearrange("p r f -> p (r f)"),
                                               ident16[:, :])
                last.then_inc(q_stps, 1)

            def turn_start(turn):
                x_count = [pe.snap(turn * 48 + 48)] * FIRST_SLOT + [pe.snap(turn * 48 + 96)]
                w_count = [pe.snap(turn * 16 + 16)] * FIRST_SLOT + [pe.snap(turn * 16 + 32)]
                entries = [pe.snap(turn * (32 * PER_TILE) + 32 * (1 + u)) for u in range(PER_TILE)]
                return x_count, w_count, entries

            def phase(items, extra):
                if items[3]:
                    hidden_transpose(items[3], 0)
                if items[1]:
                    history(items[1], 3)
                    encoded(items[1], extra)
                if items[3]:
                    cell_gates(items[3], 1)
                if items[2]:
                    cell_gates(items[2], 0)
                if items[0]:
                    history_waits(items[0], items[2], extra)
                    history(items[0], 0)
                    history(items[0], 1)
                if items[3]:
                    logit_bias(items[3])
                if items[1]:
                    entry_transposes(items[1])
                if items[0]:
                    history(items[0], 2)
                if items[2]:
                    candidates_x(items[2], items[3], extra)
                if items[3]:
                    hidden_transpose(items[3], 1)
                if items[2]:
                    cell_bias(items[2], 1)
                if items[1]:
                    encoder1_now(items[1])
                if items[2]:
                    candidates_s(items[2])
                if items[3]:
                    gate_logits(items[3])
                if items[1]:
                    cell_bias(items[1], 0)
                if items[4]:
                    state_transposes(items[4])
                if items[1]:
                    encoder2(items[1])

            run_phases(pe, phase, turn_start)

        @block.scalar
        def _(act):
            load = load_by(act)

            def cell_weights(dst, src):
                load(dst[:, H:4 * H], src[:, 0:3 * H])
                load(dst[:, 0:H], src[:, 3 * H:4 * H])

            act.wait_ge(s_zero, ZEROED)
            for r in range(TILES):
                j = 2 * (r % 2) + r // 2
                top, low = slice(H * r, H * r + H), slice(CELL_IN + H * r, CELL_IN + H * r + H)
                load(enc2_bias[top, :], w["enc_b2"].rearrange("(e o) -> e o", o=1))
                cell_weights(cell_w[0][top, j, :], w["lstm_wih1"])
                cell_weights(cell_w[0][low, r, :], w["lstm_whh1"])
                cell_weights(cell_w[1][top, r, :], w["lstm_whh2"])
                cell_weights(cell_w[1][low, r, :], w["lstm_wih2"])
                for n in range(2):
                    at = (n * TILES + r) * 4 * H
                    cell_weights(bias_row[0:1, at:at + 4 * H],
                                 w[f"lstm_b{n + 1}"].rearrange("(o a) -> o a", o=1))
                load(gate_w[top, r, :], w["gate_w"])
                at = 2 * CELL_COLS + C * r
                load(bias_row[0:1, at:at + C], w["gate_b"].rearrange("(o a) -> o a", o=1))
            assert loads[0] == LOADS
            act.wait_ge(s_prep, PREP_ALL)

            def encoded(item):
                g, n, u = item
                act.wait_ge(q_encps, n)
                src = chain[g][:, 0:TILES * TRAJ].rearrange("p (j f) -> p j f", j=TILES)
                nc.scalar.activation(enc[:, g, :, 0:TRAJ], src, ACT.Tanh).then_inc(q_enc, 1)

            def encoded_high(item):
                g, n, u = item
                act.wait_ge(q_encps, n)
                src = chain[g][:, 0:TILES * TRAJ].rearrange("p (j o f) -> p j o f", j=TILES, o=1)
                nc.scalar.activation(enc_parts[:, g, :, 0:PARTS:2, 0:TRAJ],
                                     src.to_broadcast([P, TILES, 2, TRAJ]), ACT.Tanh)

            def entry(item):
                g, n, u = item
                act.wait_ge(q_inpps, n)
                nc.scalar.activation(inp_t[0:PARTS * INP, g, :], chain[g][:, :].bitcast(FP16)[0:PARTS * INP, 0:GB],
                                     ACT.Copy).then_inc(q_inp, 1)

            def encoder1(item):
                g, n, u = item
                act.wait_ge(q_aps, n)
                nc.scalar.activation(a_sb[:, g, :], a_ps[g % 2][:, 0:GB // 2], ACT.Relu,
                                     bias=enc1_bias[:, 0:1]).then_inc(q_a, 1)

            def candidates(item):
                g, n, u = item
                act.wait_ge(q_candps, n)
                nc.scalar.activation(cand[:, g, :, :, :].rearrange("p j s c -> p (j s c)"),
                                     cand_ps[:, :], ACT.Tanh).then_inc(q_cand, 1)

            def cell_gates(item, c):
                g, n, u = item
                act.wait_ge(q_cps[c], n)
                nc.scalar.activation(gates[c][:, g, :, 0:4, :],
                                     chain[g][:, OUT_AT:OUT_AT + CELL_COLS].rearrange("p (j o f) -> p j o f", j=TILES, o=4),
                                     ACT.Tanh).then_inc(q_gates[c], 1)

            def cell_tanh(item, c):
                g, n, u = item
                act.wait_ge(q_cell[c], n)
                nc.scalar.activation(tanh_c[c][:, g, :, :], gates[c][:, g, :, 4, :], ACT.Tanh, scale=0.5)\
                    .then_inc(q_tanhc[c], 1)

            def cell_input(item):
                g, n, u = item
                act.wait_ge(q_cinps, n)
                nc.scalar.activation(cell_in[0][0:CELL_IN, g, :], chain[g][0:CELL_IN, 0:P], ACT.Relu,
                                     bias=enc2_bias[:, 0:1]).then_inc(q_cin, 1)

            def take_hidden(item, c):
                g, n, u = item
                rows = slice(CELL_IN * (1 - c), CELL_IN * (1 - c) + CELL_IN)
                act.wait_ge(q_hps[c], n)
                nc.scalar.activation(cell_in[1][rows, g, :], chain[g][rows, 0:P], ACT.Copy)\
                    .then_inc(q_ht[c], 1)

            def next_hidden(item):
                g, n, u = item
                act.wait_ge(q_ht[0], n)
                rows = slice(CELL_IN, 2 * CELL_IN)
                nc.scalar.activation(cell_in[0][rows, g, :], cell_in[1][rows, g, :], ACT.Copy)\
                    .then_inc(q_hnext, 1)

            def exponentials(item):
                g, n, u = item
                act.wait_ge(q_logit, n)
                nc.scalar.activation(expd[:, g, :, :], logit[:, g, :, :], ACT.Exp).then_inc(q_exp, 1)

            def phase(items, extra):
                if items[3]:
                    cell_tanh(items[3], 1)
                if items[2]:
                    cell_gates(items[2], 0)
                if items[1]:
                    entry(items[1])
                if items[3]:
                    take_hidden(items[3], 1)
                if items[1]:
                    encoder1(items[1])
                if items[2]:
                    cell_tanh(items[2], 0)
                if items[3]:
                    exponentials(items[3])
                if items[2]:
                    take_hidden(items[2], 0)
                if items[1]:
                    cell_input(items[1])
                if items[3]:
                    next_hidden(items[3])
                if items[0]:
                    encoded_high(items[0])
                    encoded(items[0])
                if items[2]:
                    cell_gates(items[2], 1)
                    candidates(items[2])

            run_phases(act, phase)

        @block.vector
        def _(dve):
            V = nc.vector
            V.memset(ones[:, :], 1.0)
            V.memset(x_stage[:, :], 0.0).then_inc(s_zero, 1)
            V.memset(enc1_stage[:, :, :], 0.0).then_inc(s_zero, 1)
            for n in range(2):
                V.memset(cell_w[n][:, :, :], 0.0)
            V.memset(gate_w[:, :, :], 0.0)
            V.memset(w_enc2[:, :], 0.0).then_inc(s_zero, 1)
            V.memset(err_ring[:, :, :], 0.5).then_inc(s_zero, 1)
            V.memset(cell_in[0][CELL_IN:2 * CELL_IN, :, :], 0.0).then_inc(q_hnext, GROUPS)
            V.memset(cell_in[1][0:CELL_IN, :, :], 0.0).then_inc(q_ht[1], GROUPS)
            V.memset(h[1], 0.0)
            for n in range(2):
                V.memset(gates[n][:, :, :, 4, :], 0.0)
            V.memset(xs[96:P, :, :], 1.0)
            V.memset(ones16[:, :], 1.0)
            V.memset(hist[:, :, :, :].rearrange("p a k b -> p (a k b)").bitcast(FP32), 0.0)
            V.memset(state_t[:, :, :], 0.0).then_inc(q_st, GROUPS)
            dve.wait_ge(q_st, GROUPS)
            dve.wait_ge(s_load, LOADS)

            steps = [0]

            def link(ins):
                steps[0] += 1
                ins.then_inc(s_prep, 1)
                dve.wait_ge(s_prep, steps[0])

            def by_source(stage):
                return stage.rearrange("p (c s) -> p s c", c=C)

            def high_parts(high, stage, rows):
                V.tensor_copy(high[rows, 0:NS].rearrange("p (s c) -> p s c", c=C),
                              by_source(stage[rows, 0:NS]))
                link(V.tensor_copy(high[rows, NS:], stage[rows, NS:]))

            high_parts(w_s, s_stage, slice(0, PARTS * S))
            high_parts(w_x, x_stage, slice(0, P))
            for low, high, stage, rows in ((w_s, w_s, s_stage, slice(64, 96)),
                                           (bias_low, w_x, x_stage, slice(96, P)),
                                           (w_x, w_x, x_stage, slice(64, 96))):
                V.tensor_tensor(low[rows, 0:NS].rearrange("p (s c) -> p s c", c=C),
                                by_source(stage[rows, 0:NS]),
                                high[rows, 0:NS].rearrange("p (s c) -> p s c", c=C), ALU.subtract)
                link(V.tensor_tensor(low[rows, NS:], stage[rows, NS:], high[rows, NS:], ALU.subtract))
            for start in range(0, TABLE, MEM):
                m = min(MEM, TABLE - start)
                link(V.tensor_copy(enc1_table[:, start:start + m, 0, :], enc1_stage[:, 0:m, :]))
                link(V.tensor_tensor(enc1_table[:, start:start + m, 1, :], enc1_stage[:, 0:m, :],
                                     enc1_table[:, start:start + m, 0, :], ALU.subtract))
            link(V.tensor_copy(now_parts[0:INP, 0, :], now_stage[0:INP, 0, :]))
            link(V.tensor_tensor(now_parts[0:INP, 1, :], now_stage[0:INP, 0, :],
                                 now_parts[0:INP, 0, :], ALU.subtract))
            for n, scale in enumerate((row_scale0, 0.5)):
                link(V.tensor_scalar(cell_w[n][:, :, :], cell_w[n][:, :, :], scale, None, ALU.mult))
                link(V.tensor_scalar(cell_w[n][:, :, 0:3 * H], cell_w[n][:, :, 0:3 * H], 0.5, None, ALU.mult))
            link(V.tensor_scalar(gate_w[:, :, :], gate_w[:, :, :], 0.5, None, ALU.mult))
            rows = bias_row[0:1, 0:2 * CELL_COLS].rearrange("p (j o) -> p j o", o=4 * H)
            link(V.tensor_scalar(rows[:, :, 0:3 * H], rows[:, :, 0:3 * H], 0.5, None, ALU.mult))
            link(V.tensor_copy(bias_parts[0:1, :], bias_row[0:1, :]))
            link(V.tensor_tensor(bias_low_row[0:1, :], bias_row[0:1, :], bias_parts[0:1, :], ALU.subtract))
            link(V.tensor_copy(ident16[:, :], ident[:, :]))
            V.tensor_scalar(hist[:, 0, :, :].rearrange("p k b -> p (k b)"),
                            hist[:, 0, :, :].rearrange("p k b -> p (k b)"),
                            err_rows, None, ALU.add).then_inc(s_prep, 1)
            assert steps[0] == PREP_PARTS
            first_error = err_ring[:, :, 0].rearrange("p (g j) -> p g j", g=GROUPS)
            V.tensor_copy(enc[:, :, :, TRAJ], first_error).then_inc(s_prep, 1)
            V.tensor_copy(enc_parts[:, :, :, 0, TRAJ], first_error).then_inc(s_prep, 1)
            V.tensor_copy(enc_parts[:, :, :, 2, TRAJ], first_error).then_inc(s_prep, 1)
            dve.wait_ge(s_prep, PREP_ALL)
            for place, before_first in enumerate((q_errh, q_ring, q_gate)):
                V.tensor_copy(share[:, place, :], ones[:, :]).then_inc(before_first, GROUPS)

            def error_sum(item):
                g, n, u = item
                dve.wait_ge(q_ring, n)
                V.tensor_reduce(err_sum[:, g, :], err_ring[:, TILES * g:TILES * g + TILES, :], AX,
                                ALU.add, apply_absolute_value=True).then_inc(q_errsum, 1)

            def thetas(item):
                g, n, u = item
                dve.wait_ge(q_errsum, n)
                V.tensor_scalar(theta[:, g, :], err_sum[:, g, :], 2.5 / WINDOW, 1.0, ALU.mult, ALU.min)\
                    .then_inc(q_theta, 1)

            def entry_low(item):
                g, n, u = item
                dve.wait_ge(q_enc, n)
                dve.wait_ge(q_errh, n)
                V.tensor_tensor(enc_parts[:, g, :, 1, :], enc[:, g, :, :], enc_parts[:, g, :, 0, :],
                                ALU.subtract).then_inc(q_encl, 1)

            def cell_terms(item, c):
                g, n, u = item
                dve.wait_ge(q_gates[c], n)
                V.scalar_tensor_tensor(added[c][:, g, :, :, :], gates[c][:, g, :, 1:3, :], 1.0,
                                       gates[c][:, g, :, 3:5, :], ALU.add, ALU.mult)\
                    .then_inc(q_added[c], 1)

            def cell_value(item, c):
                g, n, u = item
                dve.wait_ge(q_added[c], n)
                V.scalar_tensor_tensor(gates[c][:, g, :, 4, :], added[c][:, g, :, 1, :], 0.5,
                                       added[c][:, g, :, 0, :], ALU.mult, ALU.add).then_inc(q_cell[c], 1)

            def new_hidden(item, c):
                g, n, u = item
                dve.wait_ge(q_tanhc[c], n)
                V.scalar_tensor_tensor(h[c][:, g, :, :], gates[c][:, g, :, 0, :], 1.0,
                                       tanh_c[c][:, g, :, :], ALU.add, ALU.mult).then_inc(q_h[c], 1)

            def over_c(t, g):
                return t[:, g, :].rearrange("p (j o) -> p j o", o=1).to_broadcast([P, TILES, C])

            def logits_of(g):
                return chain[g][:, OUT_AT:OUT_AT + TILES * C].rearrange("p (j c) -> p j c", c=C)

            def peaks(item):
                g, n, u = item
                dve.wait_ge(q_logps, n)
                V.tensor_reduce(peak[:, g, :], logits_of(g), AX, ALU.max).then_inc(q_peak, 1)

            def below_peak(item):
                g, n, u = item
                dve.wait_ge(q_peak, n)
                V.tensor_tensor(logit[:, g, :, :], logits_of(g), over_c(peak, g), ALU.subtract)\
                    .then_inc(q_logit, 1)

            def totals(item):
                g, n, u = item
                dve.wait_ge(q_exp, n)
                V.tensor_reduce(total[:, g, :], expd[:, g, :, :], AX, ALU.add).then_inc(q_total, 1)

            def weighted_by_theta(item):
                g, n, u = item
                dve.wait_ge(q_exp, n)
                V.tensor_tensor(weighted[:, g, :, :], expd[:, g, :, :], over_c(theta, g), ALU.mult)

            def shares(item):
                g, n, u = item
                dve.wait_ge(q_total, n)
                V.reciprocal(share[:, g, :], total[:, g, :]).then_inc(q_share, 1)

            def fresh_gate(item):
                g, n, u = item
                dve.wait_ge(q_share, n)
                V.tensor_tensor(fresh[:, g, :, :], weighted[:, g, :, :], over_c(share, g), ALU.mult)\
                    .then_inc(q_fresh, 1)

            def new_gate(item):
                g, n, u = item
                dve.wait_ge(q_fresh, n)
                dve.wait_ge(q_kept, n)
                V.tensor_tensor(gate[:, g, :, :], fresh[:, g, :, :], kept[:, g, :, :], ALU.add)\
                    .then_inc(q_gate, 1)

            def mix(item):
                g, n, u = item
                dve.wait_ge(q_gate, n + GROUPS)
                j = slice(0, MIX_V)
                V.tensor_tensor(mixed[:, g % 2, j, :, :], cand[:, g, j, :, :], over_s(gate, g, j), ALU.mult)\
                    .then_inc(q_mixv, 1)

            def sum_own(item):
                g, n, u = item
                dve.wait_ge(q_mixv, n)
                V.tensor_reduce(state[:, g, 0:MIX_V, :], mixed[:, g % 2, 0:MIX_V, :, :], AX, ALU.add)\
                    .then_inc(q_sumv, 1)

            def sum_pool(item):
                g, n, u = item
                dve.wait_ge(q_mixp, n)
                V.tensor_reduce(state[:, g, MIX_V:TILES, :], mixed[:, g % 2, MIX_V:TILES, :, :], AX, ALU.add)\
                    .then_inc(q_sump, 1)

            def state_high(item):
                g, n, u = item
                dve.wait_ge(q_sump, n)
                twice = state[:, g, :, :].rearrange("p j (o s) -> p j o s", o=1).to_broadcast([P, TILES, 2, S])
                V.tensor_copy(state_parts[:, g, :, 0:PARTS:2, :], twice).then_inc(q_sh, 1)

            def state_low(item):
                g, n, u = item
                dve.wait_ge(q_sh, n)
                V.tensor_tensor(state_parts[:, g, :, 1, :], state[:, g, :, :], state_parts[:, g, :, 0, :],
                                ALU.subtract).then_inc(q_sl, 1)

            def prediction(item):
                g, n, u = item
                dve.wait_ge(q_sump, n)
                V.tensor_scalar(pred_now[:, g, :], state[:, g, :, S - 1], 1.0, 0.0, ALU.min, ALU.max)\
                    .then_inc(q_pred, 1)

            def state_take(item):
                g, n, u = item
                dve.wait_ge(q_stps, n)
                rows = slice(0, PARTS * S)
                V.tensor_copy(state_t[rows, g, :], chain[g][:, :].bitcast(FP16)[rows, 0:GB]).then_inc(q_st, 1)

            def phase(items, extra):
                if items[2]:
                    cell_terms(items[2], 1)
                if items[0]:
                    entry_low(items[0])
                if items[2]:
                    cell_value(items[2], 1)
                if items[3]:
                    sum_own(items[3])
                if items[2]:
                    new_hidden(items[2], 1)
                if items[3]:
                    sum_pool(items[3])
                if items[1]:
                    cell_terms(items[1], 0)
                if items[3]:
                    state_high(items[3])
                if items[1]:
                    cell_value(items[1], 0)
                if items[3]:
                    state_low(items[3])
                if items[1]:
                    thetas(items[1])
                if items[2]:
                    peaks(items[2])
                if items[1]:
                    new_hidden(items[1], 0)
                if items[2]:
                    below_peak(items[2])
                if items[3]:
                    prediction(items[3])
                    state_take(items[3])
                if items[2]:
                    totals(items[2])
                    weighted_by_theta(items[2])
                    shares(items[2])
                    fresh_gate(items[2])
                    new_gate(items[2])
                if items[0]:
                    error_sum(items[0])
                if items[2]:
                    mix(items[2])

            run_phases(dve, phase)

        @block.gpsimd
        def _(pool):
            G = nc.gpsimd
            pool.wait_ge(s_load, LOADS)
            G.tensor_copy(xh_b[0:D_IN, :], x_b[0:D_IN, :]).then_inc(s_xhb, 1)
            pool.wait_ge(s_xhb, 1)
            G.tensor_tensor(xl_b[0:D_IN, :], x_b[0:D_IN, :], xh_b[0:D_IN, :], ALU.subtract).then_inc(s_xlb, 1)

            def x_high(dst, src, k, done):
                cols = slice(512 * k, 512 * k + 512)
                parts = src.shape[0]
                G.tensor_tensor(dst[:, cols], src[:, cols], ones[0:parts, 0:1].to_broadcast([parts, 512]),
                                ALU.mult).then_inc(done, 1)

            def x_low(dst, src, high, k, done):
                cols = slice(512 * k, 512 * k + 512)
                G.tensor_tensor(dst[:, cols], src[:, cols], high[:, cols], ALU.subtract).then_inc(done, 1)

            for k in range(4):
                x_high(xh_a, x_a, k, s_xha)
            for k in range(4):
                pool.wait_ge(s_xha, k + 1)
                x_low(xl_a, x_a, xh_a, k, s_xla)
            pool.wait_ge(s_xb, 16)
            pool.wait_ge(s_xs[FIRST_SLOT], 48)
            for k in range(4):
                x_high(xh_b, x_b, k, s_xhb)
            for k in range(4):
                pool.wait_ge(s_xhb, k + 2)
                x_low(xl_b, x_b, xh_b, k, s_xlb)
            pool.wait_ge(s_prep, PREP_ALL)

            def kept_share(item):
                g, n, u = item
                pool.wait_ge(q_theta, n)
                G.tensor_tensor(one_theta[:, g, :], ones[:, :], theta[:, g, :], ALU.subtract)\
                    .then_inc(q_onetheta, 1)

            def kept_gate(item):
                g, n, u = item
                pool.wait_ge(q_onetheta, n)
                G.tensor_tensor(kept[:, g, :, :], gate[:, g, :, :],
                                one_theta[:, g, :].rearrange("p (j o) -> p j o", o=1)
                                .to_broadcast([P, TILES, C]), ALU.mult).then_inc(q_kept, 1)

            def mix(item):
                g, n, u = item
                pool.wait_ge(q_gate, n + GROUPS)
                j = slice(MIX_V, TILES)
                G.tensor_tensor(mixed[:, g % 2, j, :, :], cand[:, g, j, :, :], over_s(gate, g, j), ALU.mult)\
                    .then_inc(q_mixp, 1)

            def place(item, extra):
                g, n, u = item
                if extra is None:
                    return 0, 1
                if extra == "end":
                    return STEPS - 1, STEPS % WINDOW
                step, odd, even = extra[:3]
                after = u + 2
                return step + (u + 1), (odd + after if after < PER_TILE else even + (after - PER_TILE))

            def new_error(item, extra):
                g, n, u = item
                tiles = slice(TILES * g, TILES * g + TILES)
                step, ring = place(item, extra)
                pool.wait_ge(q_pred, n)
                pred = pred_now[:, g, :].rearrange("p (j o) -> p j o", o=1)
                G.tensor_tensor(enc[:, g, :, TRAJ:INP], pred, ys[:, tiles, bass.ds(step, 1)], ALU.subtract)\
                    .then_inc(q_err, 1)

            def error_high(item):
                g, n, u = item
                pool.wait_ge(q_err, n)
                twice = enc[:, g, :, TRAJ:INP].to_broadcast([P, TILES, 2])
                every = ones[:, :].rearrange("p (j o) -> p j o", o=1).to_broadcast([P, TILES, 2])
                G.tensor_tensor(enc_parts[:, g, :, 0:PARTS:2, TRAJ], twice, every, ALU.mult)\
                    .then_inc(q_errh, 1)

            def keep_results(item, extra):
                g, n, u = item
                tiles = slice(TILES * g, TILES * g + TILES)
                step, ring = place(item, extra)
                pred = pred_now[:, g, :].rearrange("p (j o) -> p j o", o=1)
                G.tensor_copy(preds[:, tiles, bass.ds(step, 1)], pred).then_inc(q_predout, 1)
                G.tensor_copy(err_ring[:, tiles, bass.ds(ring, 1)], enc[:, g, :, TRAJ:INP])\
                    .then_inc(q_ring, 1)

            def turn_start(turn):
                step = pool.snap(turn * PER_TILE)
                odd = pool.snap((turn % 2) * PER_TILE)
                even = pool.snap((turn + 1) % 2 * PER_TILE)
                loaded = pool.snap(turn * 16 + 16)
                fours = pool.snap(turn * 4)
                spreads = pool.snap(turn * 48 + 48)
                return step, odd, even, loaded, fours, spreads

            def x_parts(new, extra):
                k, n, u = new
                step, odd, even, loaded, fours, spreads = extra
                if u == 1:
                    if k == 0:
                        pool.wait_ge(s_xa, loaded)
                        for v in range(AHEAD_A):
                            pool.wait_ge(s_xs[v], spreads)
                    x_high(xh_a, x_a, k, s_xha)
                elif u == 2:
                    pool.wait_ge(s_xha, fours + (k + 5))
                    x_low(xl_a, x_a, xh_a, k, s_xla)
                elif u == 3:
                    if k == 0:
                        pool.wait_ge(s_xb, loaded + 16)
                        for v in range(AHEAD_B):
                            pool.wait_ge(s_xs[AHEAD_A + v], spreads + 48 * v)
                    x_high(xh_b, x_b, k, s_xhb)
                elif u == 4:
                    pool.wait_ge(s_xhb, fours + (k + 6))
                    x_low(xl_b, x_b, xh_b, k, s_xlb)

            def phase(items, extra):
                if items[3]:
                    error_high(items[3])
                if items[2]:
                    mix(items[2])
                if items[0]:
                    kept_share(items[0])
                    kept_gate(items[0])
                if items[3]:
                    keep_results(items[3], extra)
                if items[2]:
                    new_error(items[2], extra)
                if items[0] and extra:
                    x_parts(items[0], extra)

            run_phases(pool, phase, turn_start)


ZEROED = 4
LOADS = 16 * (2 + 3 * 2 + 3 * 2 + 2 * 2 + (2 * PER_TILE - 1) + 2 + 4 + TILES * (1 + 4 * 2 + 2 * 2 + 2) + 5)
PREP_PARTS = 2 + 3 + 2 * 3 + 2 + 4 + 1 + 1 + 2 + 1
PREP_ALL = PREP_PARTS + 4

WEIGHTS = ("We", "Ue", "be", "Wx", "Ws", "bk", "enc_w1", "enc_b1", "enc_w2", "enc_b2", "gate_w",
           "gate_b", "lstm_wih1", "lstm_whh1", "lstm_b1", "lstm_wih2", "lstm_whh2", "lstm_b2")


def kernel(**inputs):
    import concourse.bacc as bacc
    from concourse.bass_utils import run_bass_kernel_spmd

    nc = bacc.Bacc("TRN2", target_bir_lowering=False, num_devices=1)
    arrays = {}

    def give(name, a):
        a = np.ascontiguousarray(a)
        arrays["in_" + name] = a
        return nc.dram_tensor("in_" + name, a.shape, mybir.dt.from_np(a.dtype), kind="ExternalInput").ap()

    x = np.asarray(inputs["r_x"])
    x_t = give("x_t", np.transpose(x, (1, 2, 0)).reshape(STEPS * D_IN, BATCH))
    y = give("y", inputs["r_y"])
    error0 = give("error0", inputs["r_error0"])
    gate0 = give("gate0", inputs["r_gate0"])
    w = {n: give(n, inputs[f"L0_rec_{n}"]) for n in WEIGHTS}
    row = np.arange(P)
    columns = np.zeros((P, 2), np.float32)
    columns[:, 0] = np.where(row < CELL_IN, 1.0, 0.5)
    columns[:, 1] = np.where((row % INP == INP - 1) & (row < HROWS), 0.5, 0.0)
    ident_c = give("ident_c", np.eye(P, dtype=np.float32))
    columns_c = give("columns_c", columns)
    out = nc.dram_tensor("preds_out", (BATCH, STEPS), FP32, kind="ExternalOutput").ap()
    recurrent_kernel(nc, x_t, y, error0, gate0, w, ident_c, columns_c, out)
    result = run_bass_kernel_spmd(nc, [arrays], core_ids=[0])
    return result.results[0]["preds_out"]
```
